# Optimizing a Trainium2 kernel written in Bass

```python
import numpy as np
import jax
import jax.numpy as jnp

def _softmax(x, axis=-1):
    return jax.nn.softmax(x, axis=axis)

def _gelu(x):
    return jax.nn.gelu(x, approximate=True)

def _silu(x):
    return jax.nn.silu(x)

def _sigmoid(x):
    return jax.nn.sigmoid(x)

def _layernorm(x, axis=-1, eps=1e-05):
    m = jnp.mean(x, axis=axis, keepdims=True)
    v = jnp.var(x, axis=axis, keepdims=True)
    return (x - m) / jnp.sqrt(v + eps)

def _scatter_add(tgt, idx, src, axis=0):
    return tgt.at[idx].add(src)

def _segment_sum(src, seg, n):
    return jax.ops.segment_sum(src, seg, n)
kernel_name = 'mk_audio_tower_d1_tok_aud1d256_r4_f6013a'

def setup_inputs(seed: int=0):
    np.random.seed(seed)
    _w = jnp.asarray

    def _rec_inputs():
        import jax
        import jax.numpy as jnp
        _rk = jax.random.key(seed)
        x = 0.000296351 + 0.99907 * jax.random.normal(jax.random.fold_in(_rk, 1), (16, 4000), jnp.float32)
        return x
    x = _rec_inputs()

    def _L0_tok_setup():
        import jax, jax.numpy as jnp
        import numpy as np
        B, L = (64, 4096)
        INTERP_FACTOR = 0.25
        WINDOW, STEP = (64, 64)
        ALPHA, BETA, TEMP = (0.12, 0.9, 1.0)
        A = -0.75

        def _cubic_w(t):
            at = jnp.abs(t)
            w_near = ((A + 2.0) * at - (A + 3.0)) * at * at + 1.0
            w_far = ((A * at - 5.0 * A) * at + 8.0 * A) * at - 4.0 * A
            return jnp.where(at <= 1.0, w_near, jnp.where(at < 2.0, w_far, 0.0))

        def cubic_interpolate_1d(signal, interp_factor):
            b, n = signal.shape
            num_points = int((n - 1) / interp_factor) + 1
            x = jnp.linspace(0.0, 1.0, num_points) * (n - 1)
            i0 = jnp.floor(x).astype(jnp.int32)
            frac = x - i0.astype(x.dtype)
            offs = jnp.arange(-1, 3)
            idx = jnp.clip(i0[:, None] + offs[None, :], 0, n - 1)
            w = _cubic_w(frac[:, None] - offs[None, :].astype(x.dtype))
            taps = signal[:, idx]
            return jnp.einsum('bpk,pk->bp', taps, w)

        def _apply_kernels(x):
            poly = (x + 1.3) ** 2
            gauss = jnp.exp(-0.5 * ((x - 0.7) / 1.0) ** 2)
            return 0.5 * poly + 0.5 * gauss

        def soft_minimum(a, b, temperature):
            b = jnp.broadcast_to(b, a.shape)
            stacked = jnp.stack([-a * temperature, -b * temperature], axis=0)
            return -jax.nn.logsumexp(stacked, axis=0) / temperature

        def _forward(signal):
            interp = cubic_interpolate_1d(signal, INTERP_FACTOR)
            n = interp.shape[1]
            n_windows = (n - WINDOW) // STEP + 1
            starts = jnp.arange(n_windows) * STEP
            idx = starts[:, None] + jnp.arange(WINDOW)[None, :]
            windows = interp[:, idx]
            kw = _apply_kernels(windows)
            M = jnp.abs(jnp.fft.fft(kw, axis=-1))
            Mmax = jnp.max(M, axis=-1, keepdims=True)
            thr = ALPHA * Mmax
            mask = jax.nn.sigmoid((M - thr) * TEMP)
            Mt = M * mask
            return soft_minimum(Mt, BETA * Mmax, TEMP)
        key = jax.random.key(seed)
        return {'signal': jax.random.normal(key, (B, L), dtype=jnp.float32)}
    _L0_tok_all = _L0_tok_setup()
    _L0_tok_in = {k: v for k, v in _L0_tok_all.items() if k in ()}
    del _L0_tok_all

    def _L0_attn_setup():
        import jax, jax.numpy as jnp
        import numpy as np
        B, S, F, H = (4, 256, 64, 8)
        SCALE = float(F) ** 0.5
        key = jax.random.key(seed)
        ks = jax.random.split(key, 5)
        return {'q_input': jax.random.normal(ks[0], (B, S, F), dtype=jnp.float32), 'Wq': jax.random.normal(ks[1], (F, F * H), dtype=jnp.float32) * 0.02, 'Wk': jax.random.normal(ks[2], (F, F * H), dtype=jnp.float32) * 0.02, 'Wv': jax.random.normal(ks[3], (F, F * H), dtype=jnp.float32) * 0.02, 'Wo': jax.random.normal(ks[4], (F * H, F), dtype=jnp.float32) * 0.02}
    _L0_attn_all = _L0_attn_setup()
    _L0_attn_in = {k: v for k, v in _L0_attn_all.items() if k in ('Wq', 'Wk', 'Wv', 'Wo')}
    del _L0_attn_all

    def _L0_ffn_setup():
        import jax, jax.numpy as jnp
        import numpy as np
        B, A = (1024, 8)
        IN, OUT = (64, 64)
        SH1, SH2 = (64, 128)
        EH1, EH2 = (128, 64)
        E, TOPK = (4, 2)

        def _shared_mlp(x, W1, b1, W2, b2, W3, b3):
            h = jax.nn.relu(x @ W1 + b1)
            h = jax.nn.relu(h @ W2 + b2)
            return h @ W3 + b3

        def _experts_mlp(x, eW1, eb1, eW2, eb2, eW3, eb3):
            h = jax.nn.relu(jnp.einsum('baf,efh->ebah', x, eW1) + eb1[:, None, None, :])
            h = jax.nn.relu(jnp.einsum('ebah,ehg->ebag', h, eW2) + eb2[:, None, None, :])
            o = jnp.einsum('ebag,ego->ebao', h, eW3) + eb3[:, None, None, :]
            return jnp.moveaxis(o, 0, -1)
        key = jax.random.key(seed)
        ks = jax.random.split(key, 16)
        s = 0.05
        return {'x': jax.random.normal(ks[0], (B, A, IN), jnp.float32), 'sW1': jax.random.normal(ks[1], (IN, SH1), jnp.float32) * s, 'sb1': jnp.zeros((SH1,), jnp.float32), 'sW2': jax.random.normal(ks[2], (SH1, SH2), jnp.float32) * s, 'sb2': jnp.zeros((SH2,), jnp.float32), 'sW3': jax.random.normal(ks[3], (SH2, OUT), jnp.float32) * s, 'sb3': jnp.zeros((OUT,), jnp.float32), 'eW1': jax.random.normal(ks[4], (E, IN, EH1), jnp.float32) * s, 'eb1': jnp.zeros((E, EH1), jnp.float32), 'eW2': jax.random.normal(ks[5], (E, EH1, EH2), jnp.float32) * s, 'eb2': jnp.zeros((E, EH2), jnp.float32), 'eW3': jax.random.normal(ks[6], (E, EH2, OUT), jnp.float32) * s, 'eb3': jnp.zeros((E, OUT), jnp.float32), 'gW': jax.random.normal(ks[7], (IN, E), jnp.float32) * s, 'gb': jnp.zeros((E,), jnp.float32)}
    _L0_ffn_all = _L0_ffn_setup()
    _L0_ffn_in = {k: v for k, v in _L0_ffn_all.items() if k in ('sW1', 'sb1', 'sW2', 'sb2', 'sW3', 'sb3', 'eW1', 'eb1', 'eW2', 'eb2', 'eW3', 'eb3', 'gW', 'gb')}
    del _L0_ffn_all
    return {'x': x, 'L0_attn_Wq': _L0_attn_in['Wq'], 'L0_attn_Wk': _L0_attn_in['Wk'], 'L0_attn_Wv': _L0_attn_in['Wv'], 'L0_attn_Wo': _L0_attn_in['Wo'], 'L0_ffn_sW1': _L0_ffn_in['sW1'], 'L0_ffn_sb1': _L0_ffn_in['sb1'], 'L0_ffn_sW2': _L0_ffn_in['sW2'], 'L0_ffn_sb2': _L0_ffn_in['sb2'], 'L0_ffn_sW3': _L0_ffn_in['sW3'], 'L0_ffn_sb3': _L0_ffn_in['sb3'], 'L0_ffn_eW1': _L0_ffn_in['eW1'], 'L0_ffn_eb1': _L0_ffn_in['eb1'], 'L0_ffn_eW2': _L0_ffn_in['eW2'], 'L0_ffn_eb2': _L0_ffn_in['eb2'], 'L0_ffn_eW3': _L0_ffn_in['eW3'], 'L0_ffn_eb3': _L0_ffn_in['eb3'], 'L0_ffn_gW': _L0_ffn_in['gW'], 'L0_ffn_gb': _L0_ffn_in['gb']}

def reference(x, L0_attn_Wq, L0_attn_Wk, L0_attn_Wv, L0_attn_Wo, L0_ffn_sW1, L0_ffn_sb1, L0_ffn_sW2, L0_ffn_sb2, L0_ffn_sW3, L0_ffn_sb3, L0_ffn_eW1, L0_ffn_eb1, L0_ffn_eW2, L0_ffn_eb2, L0_ffn_eW3, L0_ffn_eb3, L0_ffn_gW, L0_ffn_gb):
    import jax
    import jax.numpy as jnp

    def _L0_tok_ref(signal):
        import jax, jax.numpy as jnp
        import numpy as np
        B, L = (64, 4096)
        INTERP_FACTOR = 0.25
        WINDOW, STEP = (64, 64)
        ALPHA, BETA, TEMP = (0.12, 0.9, 1.0)
        A = -0.75

        def _cubic_w(t):
            at = jnp.abs(t)
            w_near = ((A + 2.0) * at - (A + 3.0)) * at * at + 1.0
            w_far = ((A * at - 5.0 * A) * at + 8.0 * A) * at - 4.0 * A
            return jnp.where(at <= 1.0, w_near, jnp.where(at < 2.0, w_far, 0.0))

        def cubic_interpolate_1d(signal, interp_factor):
            b, n = signal.shape
            num_points = int((n - 1) / interp_factor) + 1
            x = jnp.linspace(0.0, 1.0, num_points) * (n - 1)
            i0 = jnp.floor(x).astype(jnp.int32)
            frac = x - i0.astype(x.dtype)
            offs = jnp.arange(-1, 3)
            idx = jnp.clip(i0[:, None] + offs[None, :], 0, n - 1)
            w = _cubic_w(frac[:, None] - offs[None, :].astype(x.dtype))
            taps = signal[:, idx]
            return jnp.einsum('bpk,pk->bp', taps, w)

        def _apply_kernels(x):
            poly = (x + 1.3) ** 2
            gauss = jnp.exp(-0.5 * ((x - 0.7) / 1.0) ** 2)
            return 0.5 * poly + 0.5 * gauss

        def soft_minimum(a, b, temperature):
            b = jnp.broadcast_to(b, a.shape)
            stacked = jnp.stack([-a * temperature, -b * temperature], axis=0)
            return -jax.nn.logsumexp(stacked, axis=0) / temperature

        def _forward(signal):
            interp = cubic_interpolate_1d(signal, INTERP_FACTOR)
            n = interp.shape[1]
            n_windows = (n - WINDOW) // STEP + 1
            starts = jnp.arange(n_windows) * STEP
            idx = starts[:, None] + jnp.arange(WINDOW)[None, :]
            windows = interp[:, idx]
            kw = _apply_kernels(windows)
            M = jnp.abs(jnp.fft.fft(kw, axis=-1))
            Mmax = jnp.max(M, axis=-1, keepdims=True)
            thr = ALPHA * Mmax
            mask = jax.nn.sigmoid((M - thr) * TEMP)
            Mt = M * mask
            return soft_minimum(Mt, BETA * Mmax, TEMP)
        return _forward(signal)

    def _L0_attn_ref(q_input, Wq, Wk, Wv, Wo):
        import jax, jax.numpy as jnp
        import numpy as np
        B, S, F, H = (4, 256, 64, 8)
        SCALE = float(F) ** 0.5
        b, s, f = q_input.shape
        h = Wq.shape[1] // f
        q = (q_input.reshape(b * s, f) @ Wq).reshape(b, s, f, h)
        k = (q_input.reshape(b * s, f) @ Wk).reshape(b, s, f, h)
        v = (q_input.reshape(b * s, f) @ Wv).reshape(b, s, f, h)
        qkt = jnp.einsum('bifh,bjfh->bijh', q, k)
        attn = jax.nn.sigmoid(qkt * SCALE)
        wv = jnp.einsum('bijh,bjfh->bifh', attn, v)
        wv = wv.reshape(b * s, f * h)
        out = jax.nn.relu(wv @ Wo)
        return out.reshape(b, s, f)

    def _L0_ffn_ref(x, sW1, sb1, sW2, sb2, sW3, sb3, eW1, eb1, eW2, eb2, eW3, eb3, gW, gb):
        import jax, jax.numpy as jnp
        import numpy as np
        B, A = (1024, 8)
        IN, OUT = (64, 64)
        SH1, SH2 = (64, 128)
        EH1, EH2 = (128, 64)
        E, TOPK = (4, 2)

        def _shared_mlp(x, W1, b1, W2, b2, W3, b3):
            h = jax.nn.relu(x @ W1 + b1)
            h = jax.nn.relu(h @ W2 + b2)
            return h @ W3 + b3

        def _experts_mlp(x, eW1, eb1, eW2, eb2, eW3, eb3):
            h = jax.nn.relu(jnp.einsum('baf,efh->ebah', x, eW1) + eb1[:, None, None, :])
            h = jax.nn.relu(jnp.einsum('ebah,ehg->ebag', h, eW2) + eb2[:, None, None, :])
            o = jnp.einsum('ebag,ego->ebao', h, eW3) + eb3[:, None, None, :]
            return jnp.moveaxis(o, 0, -1)
        all_out = _experts_mlp(x, eW1, eb1, eW2, eb2, eW3, eb3)
        shared = _shared_mlp(x, sW1, sb1, sW2, sb2, sW3, sb3)
        gates = jax.nn.softmax(x @ gW + gb, axis=-1)
        topv, topi = jax.lax.top_k(gates, TOPK)
        topw = jax.nn.softmax(topv, axis=-1)
        sel = jnp.take_along_axis(all_out, topi[:, :, None, :], axis=-1)
        gated = jnp.sum(sel * topw[:, :, None, :], axis=-1)
        return shared + gated
    h = _L0_tok_ref(x)
    h = h + _L0_attn_ref(_layernorm(h, axis=-1), L0_attn_Wq, L0_attn_Wk, L0_attn_Wv, L0_attn_Wo)
    h = h + _L0_ffn_ref(_layernorm(h, axis=-1), L0_ffn_sW1, L0_ffn_sb1, L0_ffn_sW2, L0_ffn_sb2, L0_ffn_sW3, L0_ffn_sb3, L0_ffn_eW1, L0_ffn_eb1, L0_ffn_eW2, L0_ffn_eb2, L0_ffn_eW3, L0_ffn_eb3, L0_ffn_gW, L0_ffn_gb)
    return h

_drawn_inputs = setup_inputs


def setup_inputs(seed=0):
    import zlib

    import numpy as np

    out = dict(_drawn_inputs(seed))
    spreads = {'L0_ffn_sb1': (0.0, 0.8),
     'L0_ffn_sb2': (0.0, 0.8),
     'L0_ffn_sb3': (0.0, 2.0),
     'L0_ffn_eb1': (0.0, 0.8),
     'L0_ffn_eb2': (0.0, 0.8),
     'L0_ffn_eb3': (0.0, 2.0),
     'L0_ffn_gb': (0.0, 0.8)}
    factors = {'L0_ffn_sW1': 8.0,
     'L0_ffn_sW2': 8.0,
     'L0_ffn_sW3': 8.0,
     'L0_ffn_eW1': 8.0,
     'L0_ffn_eW2': 8.0,
     'L0_ffn_eW3': 8.0,
     'L0_ffn_gW': 8.0}
    for name, (base, spread) in spreads.items():
        noise = np.random.default_rng([zlib.crc32(name.encode()), seed]).standard_normal(out[name].shape)
        drawn = base * np.exp(spread * noise) if base else spread * noise
        out[name] = jnp.asarray(drawn.astype(out[name].dtype))
    for name, factor in factors.items():
        out[name] = (out[name] * factor).astype(out[name].dtype)
    return out
```

```python
from contextlib import ExitStack

import numpy as np
import concourse.bass as bass
from concourse import mybir

ALU = mybir.AluOpType
ACT = mybir.ActivationFunctionType
F32 = mybir.dt.float32
F16 = mybir.dt.float16
AX_X = mybir.AxisListType.X

NB, NS = 16, 4000
UP, WIN = 4, 64
HOP = WIN // UP
NW = (UP * (NS - 1) + 1 - WIN) // WIN + 1
P = (NW + 1) // 2
TAP = 2 * HOP + 3
NBIN = WIN // 2 + 1
F, H, E = WIN, 8, 4
R = F // 2
NG = NB // 2
TB = 2 * P
TG = 2 * TB
QSCALE = 64.0
SCORE_SCALE = float(F) ** 0.5 / QSCALE
ALPHA, BETA = 0.12, 0.9
EPS = 1e-5



def columns(sizes):
    at, out = 0, {}
    for name, n in sizes:
        out[name] = (at, at + n)
        at += n
    return out, at


CF, NCF = columns([("ident", 128), ("interp", 128), ("dft", 128), ("fold4", 128), ("minus_low", 1)])
CH, NCH = columns([("ident", 128), ("spread", 4 * 128)])
WA, NWA = columns([("q", H * F), ("k", H * F), ("v", H * F), ("o", H * F)])
WF, NWF = columns([("w1", E * 128 + 128), ("gate", E), ("w2", E * F), ("w2s", 128), ("w3", 3 * F),
                   ("b1", E + 1), ("b2", 3), ("gb", E), ("b3", 2 * F)])
NV = 4 * E + 2


def constants():
    a = -0.75
    cf = np.zeros((128, NCF), np.float32)
    cf[:, slice(*CF["ident"])] = np.eye(128)
    for c in range(2):
        for i in range(HOP):
            for j in range(UP):
                for k in range(4):
                    t = abs(j / UP - (k - 1))
                    w = ((a + 2) * t - (a + 3)) * t * t + 1 if t <= 1 else ((a * t - 5 * a) * t + 8 * a) * t - 4 * a
                    cf[c * HOP + i + k, CF["interp"][0] + c * WIN + UP * i + j] += w
    n = np.arange(WIN)
    for c in range(2):
        at = CF["dft"][0] + c * WIN
        for k in range(NBIN):
            cf[c * WIN + n, at + k] = np.cos(2 * np.pi * n * k / WIN)
        for k in range(1, NBIN - 1):
            cf[c * WIN + n, at + NBIN + k - 1] = np.sin(2 * np.pi * n * k / WIN)
    for r in range(4):
        at = CF["fold4"][0] + r * R
        for k in range(R):
            cf[k, at + k] += 1
            cf[R, at + k] -= 2 if k else 1
            if k:
                cf[F - k, at + k] += 1
    for c in range(2):
        for v in range(2, 4):
            cf[c * NV + v * E:c * NV + v * E + E, CF["minus_low"][0]] = -1
        cf[c * NV + 4 * E + 1, CF["minus_low"][0]] = -1
    ch = np.zeros((128, NCH), np.float16)
    ch[:, slice(*CH["ident"])] = np.eye(128)
    for pair in range(2):
        for c in range(2):
            for v in range(2):
                for e in range(2):
                    at = CH["spread"][0] + (2 * pair + c) * 128 + e * F
                    ch[c * NV + v * E + 2 * pair + e, at:at + F] = 1
    return cf, ch


def build(nc, x, cf_in, ch_in, wa_in, wf_in, out, y_dram):
    with ExitStack() as ctx:
        def sb(name, shape, dt=F32):
            return ctx.enter_context(nc.sbuf_tensor(name, shape, dt))

        def sem(name):
            return ctx.enter_context(nc.semaphore(name))

        cf = sb("cf", [128, NCF])
        ch = sb("ch", [128, NCH], F16)
        wa = sb("wa", [F, NWA])
        wf = sb("wf", [128, NWF])
        taps = sb("taps", [P, NB, TAP])
        area = sb("area", [128, 3 * NB * P + 2 * NB * F])
        tapsT = area[:, 0:NB * P]
        poly = area[:, NB * P:2 * NB * P]
        gauss = area[:, 2 * NB * P:3 * NB * P]
        spec2 = area[0:P, 3 * NB * P:].rearrange("p (t f) -> p t f", f=F)
        H1 = area[:, 0:2 * (E + 1) * TG].rearrange("p (s e n) -> p s e n", s=2, e=E + 1)
        H2 = area[:, 2 * (E + 1) * TG:2 * (E + 4) * TG].rearrange("p (s k n) -> p s k n", s=2, k=3)
        mag = sb("mag", [P, NB * 2, NBIN])
        masked = sb("masked", [P, NB * 2, NBIN])
        dist = sb("dist", [P, NB * 2, NBIN])
        tok = sb("tok", [P, NB * 2, F])
        peak = sb("peak", [P, 6, NB * 2])
        xn = sb("xn", [P, NB * 2, R])
        xs = sb("xs", [P, NB * 2, 4 * R], F16)
        half_neg = sb("half_neg", [128, NB * 2])
        wqT = sb("wqT", [F, H, 128])
        wkT = sb("wkT", [F, H, R])
        wvT = sb("wvT", [F, H, R])
        scoreW = sb("scoreW", [128, H * R], F16)
        outW = sb("outW", [128, 2, F])
        XT = sb("XT", [128, 3, TG], F16)
        YP = sb("YP", [128, 2, 4, TG], F16)
        YS = sb("YS", [128, 3, H, TG], F16)
        xg = sb("xg", [P, 2, 4, R])
        probs = sb("probs", [P, 3, 4, TB])
        ZS = sb("ZS", [128, 2, 2, TG])
        AO = sb("AO", [128, TB])
        h2 = sb("h2", [P, NB * 2, F])
        ln = sb("ln", [P, 4, F])
        lnsq = sb("lnsq", [P, 4, F])
        lnst = sb("lnst", [P, 6, 4])
        x2 = sb("x2", [P, 4, F])
        x2s = sb("x2s", [P, 2, 4, 2 * F], F16)
        X2T = sb("X2T", [128, NG, TG], F16)
        w1h = sb("w1h", [128, E * 128 + 128 + E], F16)
        w1l = sb("w1l", [128, E * 128 + 128 + E], F16)
        b3h = sb("b3h", [2 * NV, 2 * F], F16)
        b3s = sb("b3s", [2 * NV, 2 * F], F16)
        gt = sb("gt", [P, 4, NB * 2, E])
        gs = sb("gs", [P, 8, NB * 2])
        w16 = sb("w16", [P, NB, 2 * NV], F16)
        WT = sb("WT", [2 * NV, NB, P], F16)
        H2r = sb("H2r", [128, 2, 2, TG])
        FO = sb("FO", [128, TB])
        res = sb("res", [P, 2, 2, 2, F])

        ps = ctx.enter_context(nc.psum_tensor("ps", [128, 8, 512], F32))

        def half_bank(n, rows, tiles):
            return ps[0:rows, n, :].bitcast(F16)[:, 0:tiles * 128].rearrange("p (t n) -> p t n", t=tiles)

        ident = cf[:, slice(*CF["ident"])]
        ident16 = ch[:, slice(*CH["ident"])]

        const_in, const16_in, attn_w_in, ffn_w_in = (sem(s) for s in ("const_in", "const16_in", "attn_w_in", "ffn_w_in"))
        taps_in = [sem(f"taps_in{q}") for q in range(4)]
        tapsT_mm, tapsT_cp, pad_set, interp_mm = (sem(s) for s in ("tapsT_mm", "tapsT_cp", "pad_set", "interp_mm"))
        poly_done, gauss_done, kern_done, gsq_done = (sem(s) for s in ("poly_done", "gauss_done", "kern_done", "gsq_done"))
        dft_mm, sq_done, act1, dve1, pool1 = (sem(s) for s in ("dft_mm", "sq_done", "act1", "dve1", "pool1"))
        wfold_mm, wfold_cp, wprod_mm, wprod_cp = (sem(s) for s in ("wfold_mm", "wfold_cp", "wprod_mm", "wprod_cp"))
        xs_done, half_set = sem("xs_done"), sem("half_set")
        xt_mm, xt_cp, y_mm, y_hi, y_lo = (sem(s) for s in ("xt_mm", "xt_cp", "y_mm", "y_hi", "y_lo"))
        y_out = [sem(f"y_out{i}") for i in range(2)]
        y_in = [sem(f"y_in{i}") for i in range(3)]
        xg_cp = sem("xg_cp")
        s_mm, s_act, z_mm, z_cp = (sem(s) for s in ("s_mm", "s_act", "z_mm", "z_cp"))
        ao_mm, ao_cp, ta_mm, h2_done = (sem(s) for s in ("ao_mm", "ao_cp", "ta_mm", "h2_done"))
        ln_dve, ln_pool, x2s_done, x2t_mm, x2t_cp = (sem(s) for s in ("ln_dve", "ln_pool", "x2s_done", "x2t_mm", "x2t_cp"))
        w1_split, gate_mm, gate_dve, gate_act = (sem(s) for s in ("w1_split", "gate_mm", "gate_dve", "gate_act"))
        route_done, wt_mm, wt_cp = (sem(s) for s in ("route_done", "wt_mm", "wt_cp"))
        l1_mm, l1_act, l1_dve, l2_mm, l2_act = (sem(s) for s in ("l1_mm", "l1_act", "l1_dve", "l2_mm", "l2_act"))
        wb_mm, mix_done, l3_mm, fo_cp, to_mm, res_done = (
            sem(s) for s in ("wb_mm", "mix_done", "l3_mm", "fo_cp", "to_mm", "res_done"))
        out_done = [sem("out_done0"), sem("out_done1")]

        block = ctx.enter_context(nc.Block())
        unit_of = [(bb, half) for bb in range(2) for half in range(2)]

        @block.sync
        def _(sp):
            for q in range(4):
                b0 = 4 * q
                with nc.allow_non_contiguous_dma(reason="overlapping windows"):
                    sp.dma_start(taps[1:P - 1, b0:b0 + 4, :],
                                 bass.AP(x.tensor, b0 * NS + 2 * HOP - 1,
                                         [[2 * HOP, P - 2], [NS, 4], [1, TAP]])).then_inc(taps_in[q], 16)
                if q == 0:
                    sp.dma_start(taps[0:1, :, 1:TAP],
                                 bass.AP(x.tensor, 0, [[0, 1], [NS, NB], [1, TAP - 1]])).then_inc(taps_in[0], 16)
                    with nc.allow_non_contiguous_dma(reason="edges"):
                        sp.dma_start(taps[0:1, :, 0:1],
                                     bass.AP(x.tensor, 0, [[0, 1], [NS, NB], [1, 1]])).then_inc(taps_in[0], 16)
                    last = NS - (2 * HOP * (P - 1) - 1)
                    sp.dma_start(taps[P - 1:P, :, 0:last],
                                 bass.AP(x.tensor, NS - last, [[0, 1], [NS, NB], [1, last]])).then_inc(taps_in[0], 16)
                    sp.dma_start(taps[P - 1:P, :, last:TAP],
                                 bass.AP(x.tensor, NS - TAP + last, [[0, 1], [NS, NB], [1, TAP - last]])
                                 ).then_inc(taps_in[0], 16)
            sp.dma_start(wf[:], wf_in).then_inc(ffn_w_in, 16)
            for g in range(NG):
                for k in range(2):
                    sp.wait_ge(y_lo, 2 * g + k + 1)
                if g >= 3:
                    sp.wait_ge(y_in[g % 3], 32 * (g // 3))
                for hh in range(4):
                    sp.dma_start(y_dram[g % 3][:, :, hh, :],
                                 YP[R * hh:R * hh + R, g % 2]).then_inc(y_out[g % 2], 16)
                sp.wait_ge(y_out[g % 2], 64 * (g // 2 + 1))
                if g >= 3:
                    sp.wait_ge(s_mm, 8 * (g - 2))
                for hl in range(2):
                    stage = y_dram[g % 3]
                    src = bass.AP(stage.tensor, stage.offset + hl * H * TG,
                                  [[0, 2], [2 * H * TG, R], [1, H * TG]])
                    sp.dma_start(YS[64 * hl:64 * hl + 64, g % 3].rearrange("p h n -> p (h n)"), src,
                                 max_dma_last_dim=8192).then_inc(y_in[g % 3], 16)
            for g in range(NG):
                sp.wait_ge(res_done, g + 1)
                for bb in range(2):
                    b = 2 * g + bb
                    sp.dma_start(out[b, 0:NW - 1, :].rearrange("(p c) f -> p c f", c=2),
                                 res[0:P - 1, g % 2, bb]).then_inc(out_done[g % 2], 16)
                sp.dma_start(out[2 * g:2 * g + 2, NW - 1, :].rearrange("(a b) f -> a b f", a=1),
                             res[P - 1:P, g % 2, :, 0, :]).then_inc(out_done[g % 2], 16)
            for k in range(2):
                sp.wait_ge(out_done[k], 48 * (NG // 2))

        @block.tensor
        def _(pe):
            mm = nc.tensor.matmul

            pe.wait_ge(const_in, 16)
            for q in range(4):
                pe.wait_ge(taps_in[q], 80 if q == 0 else 16)
                for i in range(4):
                    b = 4 * q + i
                    t = nc.tensor.transpose(ps[0:TAP, q, i * P:(i + 1) * P], taps[:, b, :], ident[0:P, 0:P])
                t.then_inc(tapsT_mm, 1)
            pe.wait_ge(pad_set, 1)
            for q in range(4):
                pe.wait_ge(tapsT_cp, q + 1)
                mm(ps[:, 4 + q, 0:4 * P], cf[:, slice(*CF["interp"])], tapsT[:, 4 * q * P:4 * (q + 1) * P],
                   start=True, stop=True).then_inc(interp_mm, 1)
            for q in range(4):
                pe.wait_ge(kern_done, q + 1)
                for i in range(4):
                    b = 4 * q + i
                    t = mm(ps[0:P, q, i * 128:(i + 1) * 128], gauss[:, b * P:(b + 1) * P], cf[:, slice(*CF["dft"])],
                           start=True, stop=True)
                t.then_inc(dft_mm, 1)
            pe.wait_ge(attn_w_in, 16)
            fold4 = cf[0:F, slice(*CF["fold4"])]
            for h in range(H):
                mm(ps[0:F, 4 + h // 4, (h % 4) * 128:(h % 4 + 1) * 128],
                   wa[:, WA["q"][0] + h:WA["q"][1]:H], fold4, start=True, stop=True)
            for h in range(H):
                mm(ps[0:F, 6, h * R:(h + 1) * R], wa[:, WA["k"][0] + h:WA["k"][1]:H], fold4[:, 0:R],
                   start=True, stop=True)
            for h in range(H):
                t = mm(ps[0:F, 7, h * R:(h + 1) * R], wa[:, WA["v"][0] + h:WA["v"][1]:H], fold4[:, 0:R],
                       start=True, stop=True)
            t.then_inc(wfold_mm, 1)
            pe.wait_ge(wfold_cp, 3)
            for h in range(H):
                mm(ps[:, 4, h * R:(h + 1) * R], wqT[:, h, :], wkT[:, h, :], start=True, stop=True)
            for h in range(H):
                at = R * (h % 4)
                t = mm(ps[at:at + R, 5, (h // 4) * F:(h // 4 + 1) * F], wvT[:, h, :],
                       wa[:, WA["o"][0] + h * F:WA["o"][0] + (h + 1) * F], start=True, stop=True)
            t.then_inc(wprod_mm, 1)

            def x_transpose(g):
                if g == 0:
                    pe.wait_ge(xs_done, 1)
                    pe.wait_ge(const16_in, 16)
                if g >= 1:
                    pe.wait_ge(xt_cp, g)
                if g >= 4:
                    pe.wait_ge(x2t_cp, g - 3)
                xt = half_bank(7, 128, 4)
                for i in range(4):
                    t = nc.tensor.transpose(xt[:, i, 0:P], xs[:, 4 * g + i, :], ident16[0:P, 0:P])
                t.then_inc(xt_mm, 1)

            def y_project(g, k):
                pe.wait_ge(xt_cp, g + 1)
                if g == 0 and k == 0:
                    pe.wait_ge(wprod_cp, 3)
                if 2 * g + k >= 1:
                    pe.wait_ge(y_lo, 2 * g + k)
                mm(ps[:, 6, 0:TG], scoreW[:, k * 128:(k + 1) * 128], XT[:, g % 3, :],
                   start=True, stop=True).then_inc(y_mm, 1)

            def scores(n):
                g, t = divmod(n, 8)
                (bb, half), cj = unit_of[t // 2], t % 2
                if t == 0:
                    pe.wait_ge(y_in[g % 3], 32 * (g // 3 + 1))
                if n >= 2:
                    pe.wait_ge(s_act, n - 1)
                for j in range(2):
                    last = mm(ps[0:P, 2 * (n % 2) + j, 0:TG].rearrange("p (h n) -> p h n", h=2),
                              XT[:, g % 3, (2 * bb + cj) * P:(2 * bb + cj + 1) * P],
                              YS[:, g % 3, 4 * half + 2 * j:4 * half + 2 * j + 2, bb * TB:(bb + 1) * TB],
                              start=True, stop=True)
                last.then_inc(s_mm, 1)

            def mix(n):
                g, t = divmod(n, 8)
                u, cj = t // 2, t % 2
                bb, half = unit_of[u]
                keys = P - cj
                pe.wait_ge(s_act, n + 1)
                if t == 0:
                    pe.wait_ge(xg_cp, g + 1)
                if cj == 0 and 4 * g + u >= 2:
                    pe.wait_ge(z_cp, 4 * g + u - 1)
                for hh in range(4):
                    last = mm(ps[R * hh:R * hh + R, 4 + half, bb * TB:(bb + 1) * TB],
                              xg[0:keys, g % 2, 2 * bb + cj, :], probs[0:keys, n % 3, hh, :],
                              start=(cj == 0), stop=(cj == 1))
                last.then_inc(z_mm, 1)

            def attn_out(g):
                pe.wait_ge(z_cp, 4 * g + 4)
                for c in range(2):
                    for half in range(2):
                        z = ZS[:, g % 2, half, :].rearrange("p (b c n) -> p b c n", b=2, c=2)[:, :, c, :]
                        last = mm(ps[F * c:F * c + F, 7, 0:TB].rearrange("p (b n) -> p b n", b=2),
                                  outW[:, half, :], z, start=(half == 0), stop=(half == 1))
                last.then_inc(ao_mm, 1)

            def attn_out_T(g):
                pe.wait_ge(ao_cp, g + 1)
                for bb in range(2):
                    last = nc.tensor.transpose(ps[0:P, 7, bb * 128:(bb + 1) * 128], AO[:, bb * P:(bb + 1) * P], ident)
                last.then_inc(ta_mm, 1)

            def x2_transpose(g):
                pe.wait_ge(x2s_done, g + 1)
                pe.wait_ge(h2_done, g + 1)
                xt = half_bank(7, 128, 4)
                for i in range(4):
                    last = nc.tensor.transpose(xt[:, i, 0:P], x2s[:, g % 2, i, :], ident16[0:P, 0:P])
                last.then_inc(x2t_mm, 1)

            for g in range(2):
                x_transpose(g)
                for k in range(2):
                    y_project(g, k)
            for n in range(8 * NG):
                g, t = divmod(n, 8)
                scores(n)
                if t == 0 and g + 2 < NG:
                    x_transpose(g + 2)
                if t == 1 and g + 2 < NG:
                    y_project(g + 2, 0)
                if t == 2 and g >= 1:
                    if g + 2 < NG:
                        pe.wait_ge(xt_cp, g + 3)
                    attn_out(g - 1)
                if t == 3 and g + 2 < NG:
                    y_project(g + 2, 1)
                if t == 4 and g >= 1:
                    attn_out_T(g - 1)
                if t == 7 and g >= 1:
                    x2_transpose(g - 1)
                if n >= 1:
                    mix(n - 1)
            mix(8 * NG - 1)
            pe.wait_ge(x2t_cp, NG - 1)
            attn_out(NG - 1)
            attn_out_T(NG - 1)
            x2_transpose(NG - 1)

            pe.wait_ge(w1_split, 2)
            pe.wait_ge(x2t_cp, NG)
            pe.wait_ge(s_act, 8 * NG)
            pe.wait_ge(z_cp, 4 * NG)
            G0 = E * 128 + 128
            for r in range(2 * NB):
                for k, w in enumerate((w1h, w1l)):
                    last = mm(ps[0:P, 6, r * E:(r + 1) * E], X2T[:, r // 4, (r % 4) * P:(r % 4 + 1) * P],
                              w[:, G0:G0 + E], start=(k == 0), stop=(k == 1))
            last.then_inc(gate_mm, 1)

            def layer1(g):
                for e in range(E + 1):
                    n = (E + 1) * g + e
                    if n >= 3:
                        pg, pu = divmod(n - 3, E + 1)
                        if pu < 3:
                            pe.wait_ge(l1_act, 3 * pg + pu + 1)
                        else:
                            pe.wait_ge(l1_dve, 2 * pg + pu - 2)
                    for k, w in enumerate((w1h, w1l)):
                        last = mm(ps[:, n % 3, 0:TG], w[:, e * 128:(e + 1) * 128], X2T[:, g, :],
                                  start=(k == 0), stop=(k == 1))
                    last.then_inc(l1_mm, 1)

            def layer2(g):
                for k in range(3):
                    n = 3 * g + k
                    if n >= 2:
                        pe.wait_ge(l2_act, n - 1)
                    if k < 2:
                        pe.wait_ge(l1_act, 3 * g + (2, 3)[k])
                        if k == 1:
                            pe.wait_ge(l1_dve, 2 * g + 1)
                        for j in range(2):
                            e = 2 * k + j
                            last = mm(ps[F * j:F * j + F, 3 + n % 2, 0:TG],
                                      wf[:, WF["w2"][0] + e * F:WF["w2"][0] + (e + 1) * F], H1[:, g % 2, e, :],
                                      start=True, stop=True)
                    else:
                        pe.wait_ge(l1_dve, 2 * g + 2)
                        last = mm(ps[:, 3 + n % 2, 0:TG], wf[:, slice(*WF["w2s"])], H1[:, g % 2, E, :],
                                  start=True, stop=True)
                    last.then_inc(l2_mm, 1)
                    if k == 0 and g == 0:
                        pe.wait_ge(wt_cp, 2)
                    if k < 2:
                        m = 2 * g + k
                        if m >= 1:
                            pe.wait_ge(mix_done, m)
                        for c in range(2):
                            at = CH["spread"][0] + (2 * k + c) * 128
                            o = ps[:, 5, 0:TG].rearrange("p (b c n) -> p b c n", b=2, c=2)[:, :, c, :]
                            last = mm(o, ch[0:2 * NV, at:at + 128], WT[:, 2 * g:2 * g + 2, :],
                                      start=True, stop=True)
                        last.then_inc(wb_mm, 1)

            def layer3(g):
                pe.wait_ge(mix_done, 2 * g + 2)
                pe.wait_ge(l2_act, 3 * g + 3)
                if g >= 1:
                    pe.wait_ge(fo_cp, g)
                for c in range(2):
                    o = ps[F * c:F * c + F, 6, 0:TB].rearrange("p (b n) -> p b n", b=2)
                    mm(o, b3s[:, c * F:(c + 1) * F], WT[:, 2 * g:2 * g + 2, :], start=True, stop=False)
                for k in range(3):
                    for c in range(2):
                        o = ps[F * c:F * c + F, 6, 0:TB].rearrange("p (b n) -> p b n", b=2)
                        r = H2[:, g % 2, k, :].rearrange("p (b c n) -> p b c n", b=2, c=2)[:, :, c, :]
                        last = mm(o, wf[:, WF["w3"][0] + k * F:WF["w3"][0] + (k + 1) * F], r,
                                  start=False, stop=(k == 2))
                last.then_inc(l3_mm, 1)

            def result_T(g):
                pe.wait_ge(fo_cp, g + 1)
                if g >= 1:
                    pe.wait_ge(res_done, g)
                for bb in range(2):
                    last = nc.tensor.transpose(ps[0:P, 7, bb * 128:(bb + 1) * 128], FO[:, bb * P:(bb + 1) * P], ident)
                last.then_inc(to_mm, 1)

            pe.wait_ge(w1_split, 3)
            layer1(0)
            pe.wait_ge(route_done, 1)
            for b in range(NB):
                wt = half_bank(6 + b // 8, 2 * NV, 8)
                last = nc.tensor.transpose(wt[:, b % 8, 0:P], w16[:, b, :], ident16[0:P, 0:P])
            last.then_inc(wt_mm, 1)
            for g in range(NG):
                if g + 1 < NG:
                    layer1(g + 1)
                layer2(g)
                layer3(g)
                if g >= 1:
                    result_T(g - 1)
            result_T(NG - 1)

        dve1_at = {}
        gate_at = {}

        class Steps:

            def __init__(self, eng, s):
                self.eng, self.s, self.n = eng, s, 0

            def done(self, ins):
                ins.then_inc(self.s, 1)
                self.n += 1
                return self.n

            def wait(self, n=None):
                self.eng.wait_ge(self.s, self.n if n is None else n)

        @block.vector
        def _(dve):
            v = nc.vector
            v.memset(tapsT, 0.0).then_inc(pad_set, 1)
            dve.wait_ge(pad_set, 1)
            for q in range(4):
                dve.wait_ge(tapsT_mm, q + 1)
                v.tensor_copy(tapsT[0:TAP, 4 * q * P:4 * (q + 1) * P], ps[0:TAP, q, 0:4 * P]).then_inc(tapsT_cp, 1)
            for q in range(4):
                cols = slice(4 * q * P, 4 * (q + 1) * P)
                dve.wait_ge(gauss_done, q + 1)
                dve.wait_ge(poly_done, q + 1)
                v.tensor_tensor(gauss[:, cols], gauss[:, cols], poly[:, cols], ALU.add).then_inc(kern_done, 1)
            st = Steps(dve, dve1)
            halves = (slice(0, NB), slice(NB, 2 * NB))

            def wide(row, rows, n=NBIN):
                return peak[:, row, rows].unsqueeze(2).broadcast_to([P, NB, n])

            for i, rows in enumerate(halves):
                dve.wait_ge(sq_done, 2 * i + 2)
                dve1_at["power", rows.start] = st.done(
                    v.tensor_tensor(spec2[:, rows, 1:NBIN - 1], spec2[:, rows, 1:NBIN - 1],
                                    spec2[:, rows, NBIN:F], ALU.add))
            for i, rows in enumerate(halves):
                dve.wait_ge(act1, i + 1)
                a = st.done(v.tensor_reduce(peak[:, 0, rows], mag[:, rows, :], AX_X, ALU.max))
                st.wait(a)
                st.done(v.tensor_scalar(peak[:, 1, rows], peak[:, 0, rows], -ALPHA, None, ALU.mult))
                a = st.done(v.tensor_scalar(peak[:, 2, rows], peak[:, 0, rows], BETA, None, ALU.mult))
                st.wait(a)
                dve1_at["over", rows.start] = st.done(
                    v.tensor_tensor(masked[:, rows, :], mag[:, rows, :], wide(1, rows), ALU.add))
            for i, rows in enumerate(halves):
                dve.wait_ge(act1, i + 3)
                a = st.done(v.tensor_tensor(masked[:, rows, :], masked[:, rows, :], mag[:, rows, :], ALU.mult))
                st.wait(a)
                dve1_at["dist", rows.start] = st.done(
                    v.tensor_tensor(dist[:, rows, :], masked[:, rows, :], wide(2, rows), ALU.subtract))
                st.done(v.tensor_tensor(masked[:, rows, :], masked[:, rows, :], wide(2, rows), ALU.min))
            for i, rows in enumerate(halves):
                dve.wait_ge(act1, i + 9)
                a = st.done(v.tensor_tensor(tok[:, rows, 0:NBIN], masked[:, rows, :], dist[:, rows, :], ALU.add))
                st.wait(a)
                st.done(v.tensor_copy(tok[:, rows, NBIN:F], tok[:, rows, NBIN - 2:0:-1]))
                a = st.done(v.tensor_reduce(peak[:, 3, rows], tok[:, rows, 0:NBIN], AX_X, ALU.add))
                st.wait(a)
                a = st.done(v.scalar_tensor_tensor(peak[:, 4, rows], peak[:, 3, rows], 2.0, tok[:, rows, 0],
                                                   ALU.mult, ALU.subtract))
                st.wait(a)
                a = st.done(v.tensor_tensor(peak[:, 3, rows], peak[:, 4, rows], tok[:, rows, R], ALU.subtract))
                st.wait(a)
                a = st.done(v.tensor_scalar(peak[:, 4, rows], peak[:, 3, rows], -1.0 / F, None, ALU.mult))
                st.wait(a)
                dve1_at["centred", rows.start] = st.done(
                    v.tensor_tensor(mag[:, rows, :], tok[:, rows, 0:NBIN], wide(4, rows), ALU.add))
            for i, rows in enumerate(halves):
                dve.wait_ge(act1, i + 11)
                a = st.done(v.tensor_reduce(peak[:, 3, rows], masked[:, rows, :], AX_X, ALU.add))
                st.wait(a)
                a = st.done(v.scalar_tensor_tensor(peak[:, 5, rows], peak[:, 3, rows], 2.0, masked[:, rows, 0],
                                                   ALU.mult, ALU.subtract))
                st.wait(a)
                a = st.done(v.tensor_tensor(peak[:, 3, rows], peak[:, 5, rows], masked[:, rows, R], ALU.subtract))
                st.wait(a)
                dve1_at["squares", rows.start] = st.done(
                    v.tensor_scalar(peak[:, 4, rows], peak[:, 3, rows], 1.0 / F, EPS, ALU.mult, ALU.add))
            dve.wait_ge(wfold_mm, 1)
            v.tensor_copy(wqT[:].rearrange("p (a h) n -> p a (h n)", a=2), ps[0:F, 4:6, :]).then_inc(wfold_cp, 1)
            v.tensor_copy(wkT[:].rearrange("p h n -> p (h n)"), ps[0:F, 6, 0:H * R]).then_inc(wfold_cp, 1)
            v.tensor_copy(wvT[:].rearrange("p h n -> p (h n)"), ps[0:F, 7, 0:H * R]).then_inc(wfold_cp, 1)
            dve.wait_ge(wprod_mm, 1)
            v.tensor_scalar(scoreW[:], ps[:, 4, 0:H * R], QSCALE, None, ALU.mult).then_inc(wprod_cp, 1)
            v.tensor_copy(outW[:].rearrange("p a f -> p (a f)"), ps[:, 5, 0:2 * F]).then_inc(wprod_cp, 1)
            dve.wait_ge(wprod_cp, 1)
            v.scalar_tensor_tensor(scoreW[F:128, :], ps[F:128, 4, 0:H * R], QSCALE, scoreW[F:128, :],
                                   ALU.mult, ALU.subtract).then_inc(wprod_cp, 1)
            for i, rows in enumerate(halves):
                dve.wait_ge(pool1, i + 1)
                a = st.done(v.tensor_tensor(xn[:, rows, :], mag[:, rows, 0:R], wide(5, rows, R), ALU.mult))
                st.wait(a)
                a = st.done(v.tensor_copy(xs[:, rows, 0:R], xn[:, rows, :]))
                st.wait(a)
                a = st.done(v.tensor_tensor(xs[:, rows, R:2 * R], xn[:, rows, :], xs[:, rows, 0:R], ALU.subtract))
                st.wait(a)
                a = st.done(v.tensor_copy(xs[:, rows, 2 * R:4 * R], xs[:, rows, 0:2 * R]))
            st.wait(a)
            v.tensor_copy(peak[:, 0, 0:1], peak[:, 0, 0:1]).then_inc(xs_done, 1)

            def x_take(g):
                dve.wait_ge(xt_mm, g + 1)
                if g >= 3:
                    dve.wait_ge(s_mm, 8 * (g - 2))
                v.tensor_copy(XT[:, g % 3, :].rearrange("p (t n) -> p t n", t=4),
                              half_bank(7, 128, 4)[:, :, 0:P]).then_inc(xt_cp, 1)

            def y_take(g, k):
                m = 2 * g + k
                dve.wait_ge(y_mm, m + 1)
                if g >= 2:
                    dve.wait_ge(y_out[g % 2], 64 * (g // 2))
                v.tensor_copy(YP[:, g % 2, k, :], ps[:, 6, 0:TG]).then_inc(y_hi, 1)
                dve.wait_ge(y_hi, m + 1)
                v.tensor_tensor(YP[:, g % 2, 2 + k, :], ps[:, 6, 0:TG], YP[:, g % 2, k, :],
                                ALU.subtract).then_inc(y_lo, 1)

            def z_take(g, u):
                bb, half = unit_of[u]
                dve.wait_ge(z_mm, 8 * g + 2 * u + 2)
                if g >= 2:
                    dve.wait_ge(ao_mm, g - 1)
                v.tensor_copy(ZS[:, g % 2, half, bb * TB:(bb + 1) * TB],
                              ps[:, 4 + half, bb * TB:(bb + 1) * TB]).then_inc(z_cp, 1)

            def ao_take(g):
                dve.wait_ge(ao_mm, g + 1)
                if g >= 1:
                    dve.wait_ge(ta_mm, g)
                v.tensor_copy(AO[:], ps[:, 7, 0:TB]).then_inc(ao_cp, 1)

            def add_attention(g):
                rows = slice(4 * g, 4 * g + 4)
                dve.wait_ge(ta_mm, g + 1)
                v.scalar_tensor_tensor(h2[:, rows, :], ps[0:P, 7, 0:4 * F].rearrange("p (t f) -> p t f", f=F), 0.0,
                                       tok[:, rows, :], ALU.max, ALU.add).then_inc(h2_done, 1)

            def norm2(g):
                rows = slice(4 * g, 4 * g + 4)
                dve.wait_ge(h2_done, g + 1)
                v.tensor_reduce(lnst[:, 0, :], h2[:, rows, :], AX_X, ALU.add).then_inc(ln_dve, 1)
                dve.wait_ge(ln_dve, 4 * g + 1)
                v.tensor_scalar(lnst[:, 1, :], lnst[:, 0, :], -1.0 / F, None, ALU.mult).then_inc(ln_dve, 1)
                dve.wait_ge(ln_dve, 4 * g + 2)
                if g >= 1:
                    dve.wait_ge(ln_pool, 5 * g)
                v.tensor_tensor(ln[:], h2[:, rows, :], lnst[:, 1, :].unsqueeze(2).broadcast_to([P, 4, F]),
                                ALU.add).then_inc(ln_dve, 1)
                dve.wait_ge(ln_pool, 5 * g + 1)
                v.tensor_reduce(lnst[:, 2, :], lnsq[:], AX_X, ALU.add).then_inc(ln_dve, 1)

            def x2_take(g):
                dve.wait_ge(x2t_mm, g + 1)
                v.tensor_copy(X2T[:, g, :].rearrange("p (t n) -> p t n", t=4),
                              half_bank(7, 128, 4)[:, :, 0:P]).then_inc(x2t_cp, 1)

            for g in range(2):
                x_take(g)
                for k in range(2):
                    y_take(g, k)
            for g in range(NG):
                if g >= 1:
                    z_take(g - 1, 3)
                if g + 2 < NG:
                    x_take(g + 2)
                    y_take(g + 2, 0)
                z_take(g, 0)
                if g >= 1:
                    ao_take(g - 1)
                if g + 2 < NG:
                    y_take(g + 2, 1)
                z_take(g, 1)
                if g >= 1:
                    add_attention(g - 1)
                    norm2(g - 1)
                z_take(g, 2)
                if g == 0:
                    dve.wait_ge(ffn_w_in, 16)
                    v.tensor_copy(w1h[:], wf[:, 0:E * 128 + 128 + E]).then_inc(w1_split, 1)
                    dve.wait_ge(w1_split, 1)
                    v.tensor_tensor(w1l[:], wf[:, 0:E * 128 + 128 + E], w1h[:], ALU.subtract).then_inc(w1_split, 1)
                    b3 = wf[0:2 * NV, slice(*WF["b3"])]
                    v.tensor_copy(b3h[:], b3).then_inc(gate_dve, 1)
                    dve.wait_ge(gate_dve, 1)
                    dve.wait_ge(const_in, 16)
                    v.scalar_tensor_tensor(b3s[:], b3h[:], cf[0:2 * NV, slice(*CF["minus_low"])], b3,
                                           ALU.mult, ALU.add).then_inc(w1_split, 1)
                if g >= 1:
                    x2_take(g - 1)
            g = NG - 1
            z_take(g, 3)
            ao_take(g)
            add_attention(g)
            norm2(g)
            x2_take(g)

            gst = Steps(dve, gate_dve)
            gst.n = 1

            def step(ins):
                gst.wait(gst.done(ins))

            def per_token(row):
                return gs[:, row].unsqueeze(2).broadcast_to([P, 2 * NB, E])

            def keep_first(t):
                step(v.tensor_tensor(gt[:, t, :, 1], gt[:, t, :, 1], gt[:, t, :, 0], ALU.is_gt))
                step(v.tensor_tensor(gs[:, 7], gt[:, t, :, 0], gt[:, t, :, 1], ALU.max))
                step(v.tensor_tensor(gt[:, t, :, 2], gt[:, t, :, 2], gs[:, 7], ALU.is_gt))
                step(v.tensor_tensor(gs[:, 7], gs[:, 7], gt[:, t, :, 2], ALU.max))
                step(v.tensor_tensor(gt[:, t, :, 3], gt[:, t, :, 3], gs[:, 7], ALU.is_gt))

            dve.wait_ge(gate_mm, 1)
            gb = wf[0:P, slice(*WF["gb"])].unsqueeze(1).broadcast_to([P, 2 * NB, E])
            step(v.tensor_tensor(gt[:, 0], ps[0:P, 6, 0:2 * NB * E].rearrange("p (t e) -> p t e", e=E), gb, ALU.add))
            step(v.tensor_reduce(gs[:, 0], gt[:, 0], AX_X, ALU.max))
            step(v.tensor_tensor(gt[:, 0], gt[:, 0], per_token(0), ALU.subtract))
            assert gst.n == 4
            dve.wait_ge(gate_act, 1)
            step(v.tensor_reduce(gs[:, 1], gt[:, 1], AX_X, ALU.add))
            step(v.reciprocal(gs[:, 2], gs[:, 1]))
            step(v.tensor_tensor(gt[:, 1], gt[:, 1], per_token(2), ALU.mult))
            step(v.tensor_reduce(gs[:, 0], gt[:, 1], AX_X, ALU.max))
            step(v.tensor_tensor(gt[:, 2], gt[:, 1], per_token(0), ALU.is_equal))
            keep_first(2)
            step(v.scalar_tensor_tensor(gt[:, 1], gt[:, 2], -2.0, gt[:, 1], ALU.mult, ALU.add))
            step(v.tensor_reduce(gs[:, 3], gt[:, 1], AX_X, ALU.max))
            step(v.tensor_tensor(gs[:, 4], gs[:, 3], gs[:, 0], ALU.subtract))
            gate_at["gap"] = gst.n
            step(v.tensor_tensor(gt[:, 3], gt[:, 1], per_token(3), ALU.is_equal))
            keep_first(3)
            dve.wait_ge(gate_act, 2)
            step(v.tensor_scalar(gs[:, 6], gs[:, 5], 1.0, None, ALU.add))
            step(v.reciprocal(gs[:, 1], gs[:, 6]))
            step(v.tensor_tensor(gs[:, 2], gs[:, 5], gs[:, 1], ALU.mult))
            step(v.tensor_tensor(gt[:, 2], gt[:, 2], per_token(1), ALU.mult))
            step(v.tensor_tensor(gt[:, 3], gt[:, 3], per_token(2), ALU.mult))
            step(v.tensor_tensor(gt[:, 0], gt[:, 2], gt[:, 3], ALU.add))
            wv = w16[:].rearrange("p b (c v) -> p (b c) v", c=2)
            step(v.tensor_copy(wv[:, :, 0:E], gt[:, 0]))
            step(v.tensor_tensor(wv[:, :, E:2 * E], gt[:, 0], wv[:, :, 0:E], ALU.subtract))
            step(v.tensor_copy(wv[:, :, 2 * E:4 * E], wv[:, :, 0:2 * E]))
            v.memset(wv[:, :, 4 * E:NV], 1.0).then_inc(route_done, 1)
            def relu1(g, e):
                n = (E + 1) * g + e
                dve.wait_ge(l1_mm, n + 1)
                if g >= 2:
                    dve.wait_ge(l2_mm, 3 * (g - 1))
                v.tensor_scalar(H1[:, g % 2, e, :], ps[:, n % 3, 0:TG], wf[:, WF["b1"][0] + e:WF["b1"][0] + e + 1],
                                0.0, ALU.add, ALU.max).then_inc(l1_dve, 1)

            def weigh(g, k):
                dve.wait_ge(l2_act, 3 * g + k + 1)
                dve.wait_ge(wb_mm, 2 * g + k + 1)
                if g >= 2:
                    dve.wait_ge(l3_mm, g - 1)
                v.tensor_tensor(H2[:, g % 2, k, :], H2r[:, g % 2, k, :], ps[:, 5, 0:TG], ALU.mult).then_inc(mix_done, 1)

            def fo_take(g):
                dve.wait_ge(l3_mm, g + 1)
                if g >= 1:
                    dve.wait_ge(to_mm, g)
                v.tensor_copy(FO[:], ps[:, 6, 0:TB]).then_inc(fo_cp, 1)

            def finish(g):
                dve.wait_ge(to_mm, g + 1)
                if g >= 2:
                    dve.wait_ge(out_done[g % 2], 48 * (g // 2))
                v.tensor_tensor(res[:, g % 2].rearrange("p b c f -> p (b c) f"),
                                ps[0:P, 7, 0:4 * F].rearrange("p (t f) -> p t f", f=F),
                                h2[:, 4 * g:4 * g + 4, :], ALU.add).then_inc(res_done, 1)

            for e in range(3, E + 1):
                relu1(0, e)
            dve.wait_ge(wt_mm, 1)
            for k in range(2):
                v.tensor_copy(WT[:, 8 * k:8 * k + 8, :], half_bank(6 + k, 2 * NV, 8)[:, :, 0:P]).then_inc(wt_cp, 1)
            for g in range(NG):
                if g + 1 < NG:
                    for e in range(3, E + 1):
                        relu1(g + 1, e)
                weigh(g, 0)
                weigh(g, 1)
                if g >= 1:
                    finish(g - 1)
                fo_take(g)
            finish(NG - 1)

        @block.scalar
        def _(act):
            act.dma_start(cf[:], cf_in).then_inc(const_in, 16)
            act.dma_start(ch[:], ch_in).then_inc(const16_in, 16)
            act.dma_start(wa[:], wa_in).then_inc(attn_w_in, 16)
            fn = nc.scalar.activation
            r = 0.5 ** 0.5
            for q in range(4):
                cols = slice(4 * q * P, 4 * (q + 1) * P)
                src = ps[:, 4 + q, 0:4 * P]
                act.wait_ge(interp_mm, q + 1)
                fn(gauss[:, cols], src, ACT.Square, bias=-0.7).then_inc(gsq_done, 1)
                fn(poly[:, cols], src, ACT.Square, bias=1.3 * r, scale=r).then_inc(poly_done, 1)
                act.wait_ge(gsq_done, q + 1)
                fn(gauss[:, cols], gauss[:, cols], ACT.Exp, bias=float(np.log(0.5)), scale=-0.5).then_inc(gauss_done, 1)
            for q in range(4):
                act.wait_ge(dft_mm, q + 1)
                fn(spec2[:, 8 * q:8 * q + 8, :], ps[0:P, q, :].rearrange("p (t f) -> p t f", f=F),
                   ACT.Square).then_inc(sq_done, 1)
            n = 0
            for rows in (slice(0, NB), slice(NB, 2 * NB)):
                act.wait_ge(dve1, dve1_at["power", rows.start])
                fn(mag[:, rows, :], spec2[:, rows, 0:NBIN], ACT.Sqrt).then_inc(act1, 1)
            for rows in (slice(0, NB), slice(NB, 2 * NB)):
                act.wait_ge(dve1, dve1_at["over", rows.start])
                fn(masked[:, rows, :], masked[:, rows, :], ACT.Sigmoid).then_inc(act1, 1)
            for rows in (slice(0, NB), slice(NB, 2 * NB)):
                act.wait_ge(dve1, dve1_at["dist", rows.start])
                fn(dist[:, rows, :], dist[:, rows, :], ACT.Abs).then_inc(act1, 1)
            for i, rows in enumerate((slice(0, NB), slice(NB, 2 * NB))):
                act.wait_ge(act1, 5 + i)
                fn(dist[:, rows, :], dist[:, rows, :], ACT.Sigmoid).then_inc(act1, 1)
            for i, rows in enumerate((slice(0, NB), slice(NB, 2 * NB))):
                act.wait_ge(act1, 7 + i)
                fn(dist[:, rows, :], dist[:, rows, :], ACT.Ln).then_inc(act1, 1)
            for i, rows in enumerate((slice(0, NB), slice(NB, 2 * NB))):
                act.wait_ge(dve1, dve1_at["centred", rows.start])
                fn(masked[:, rows, :], mag[:, rows, :], ACT.Square).then_inc(act1, 1)
            for n in range(8 * NG):
                act.wait_ge(s_mm, n + 1)
                if n >= 3:
                    act.wait_ge(z_mm, n - 2)
                fn(probs[:, n % 3].rearrange("p (j h) n -> p j (h n)", j=2), ps[0:P, 2 * (n % 2):2 * (n % 2) + 2, 0:TG],
                   ACT.Sigmoid, scale=SCORE_SCALE).then_inc(s_act, 1)
            act.wait_ge(gate_dve, 4)
            fn(gt[:, 1], gt[:, 0], ACT.Exp).then_inc(gate_act, 1)
            act.wait_ge(gate_dve, gate_at["gap"])
            fn(gs[:, 5], gs[:, 4], ACT.Exp).then_inc(gate_act, 1)

            def relu1(g, e):
                n = (E + 1) * g + e
                act.wait_ge(l1_mm, n + 1)
                if g >= 2:
                    act.wait_ge(l2_mm, 3 * (g - 1))
                fn(H1[:, g % 2, e, :], ps[:, n % 3, 0:TG], ACT.Relu,
                   bias=wf[:, WF["b1"][0] + e:WF["b1"][0] + e + 1]).then_inc(l1_act, 1)

            def relu2(g, k):
                n = 3 * g + k
                act.wait_ge(l2_mm, n + 1)
                if g >= 2:
                    act.wait_ge(l3_mm, g - 1)
                dst = H2r[:, g % 2, k, :] if k < 2 else H2[:, g % 2, 2, :]
                fn(dst, ps[:, 3 + n % 2, 0:TG], ACT.Relu,
                   bias=wf[:, WF["b2"][0] + k:WF["b2"][0] + k + 1]).then_inc(l2_act, 1)

            for e in range(3):
                relu1(0, e)
            for g in range(NG):
                if g + 1 < NG:
                    for e in range(3):
                        relu1(g + 1, e)
                for k in range(3):
                    relu2(g, k)

        @block.gpsimd
        def _(pool):
            v = nc.gpsimd
            v.memset(half_neg[:], -0.5).then_inc(half_set, 1)
            pool.wait_ge(half_set, 1)
            for rows in (slice(0, NB), slice(NB, 2 * NB)):
                pool.wait_ge(dve1, dve1_at["squares", rows.start])
                v.tensor_tensor(peak[:, 5, rows], peak[:, 4, rows], half_neg[0:P, 0:NB], ALU.pow).then_inc(pool1, 1)

            def keys(g):
                if g == 0:
                    pool.wait_ge(xs_done, 1)
                if g >= 2:
                    pool.wait_ge(z_mm, 8 * (g - 1))
                v.tensor_copy(xg[:, g % 2], xn[:, 4 * g:4 * g + 4, :]).then_inc(xg_cp, 1)

            def norm2(g):
                pool.wait_ge(ln_dve, 4 * g + 3)
                v.tensor_tensor(lnsq[:], ln[:], ln[:], ALU.mult).then_inc(ln_pool, 1)
                pool.wait_ge(ln_dve, 4 * g + 4)
                v.tensor_scalar(lnst[:, 3, :], lnst[:, 2, :], 1.0 / F, EPS, ALU.mult, ALU.add).then_inc(ln_pool, 1)
                pool.wait_ge(ln_pool, 5 * g + 2)
                v.tensor_tensor(lnst[:, 4, :], lnst[:, 3, :], half_neg[0:P, 0:4], ALU.pow).then_inc(ln_pool, 1)
                pool.wait_ge(ln_pool, 5 * g + 3)
                v.tensor_tensor(x2[:], ln[:], lnst[:, 4, :].unsqueeze(2).broadcast_to([P, 4, F]),
                                ALU.mult).then_inc(ln_pool, 1)
                pool.wait_ge(ln_pool, 5 * g + 4)
                if g >= 2:
                    pool.wait_ge(x2t_mm, g - 1)
                v.tensor_copy(x2s[:, g % 2, :, 0:F], x2[:]).then_inc(ln_pool, 1)
                pool.wait_ge(ln_pool, 5 * g + 5)
                v.tensor_tensor(x2s[:, g % 2, :, F:2 * F], x2[:], x2s[:, g % 2, :, 0:F],
                                ALU.subtract).then_inc(x2s_done, 1)

            keys(0)
            for g in range(NG):
                if g + 1 < NG:
                    keys(g + 1)
                if g >= 1:
                    norm2(g - 1)
            norm2(NG - 1)


def stacked(*blocks):
    return np.concatenate([a for a, n in blocks for _ in range(n)], axis=0)


def kernel(**inputs):
    import concourse.bacc as bacc
    from concourse.bass_utils import run_bass_kernel_spmd

    a = {k: np.asarray(v) for k, v in inputs.items()}
    ffn = {k[len("L0_ffn_"):]: v for k, v in a.items() if k.startswith("L0_ffn_")}
    f32 = np.float32

    wo = a["L0_attn_Wo"].reshape(F, H * F)
    wa = np.concatenate([a["L0_attn_Wq"], a["L0_attn_Wk"], a["L0_attn_Wv"], wo], axis=1)

    wf = np.zeros((128, NWF), f32)

    def put(name, at, rows, block):
        c0 = WF[name][0] + at
        wf[rows:rows + block.shape[0], c0:c0 + block.shape[1]] = block

    for half in range(2):
        for e in range(E):
            put("w1", e * 128, half * F, ffn["eW1"][e])
        put("w1", E * 128, half * F, ffn["sW1"])
        put("gate", 0, half * F, ffn["gW"])
    for e in range(E):
        put("w2", e * F, 0, ffn["eW2"][e])
        put("w3", (e // 2) * F, (e % 2) * F, ffn["eW3"][e])
        put("b1", e, 0, ffn["eb1"][e][:, None])
        put("b2", e // 2, (e % 2) * F, ffn["eb2"][e][:, None])
    put("w2s", 0, 0, ffn["sW2"])
    put("w3", 2 * F, 0, ffn["sW3"])
    put("b1", E, 0, ffn["sb1"][:, None])
    put("b2", 2, 0, ffn["sb2"][:, None])
    put("gb", 0, 0, np.broadcast_to(ffn["gb"][None, :], (128, E)))
    last_bias = stacked((ffn["eb3"], 4), (ffn["sb3"][None, :], 2))
    for c in range(2):
        put("b3", c * F, c * NV, last_bias)

    cf, ch = constants()
    arrays = {"x_in": np.ascontiguousarray(a["x"]), "cf_in": cf, "ch_in": ch,
              "wa_in": np.ascontiguousarray(wa), "wf_in": wf}
    nc = bacc.Bacc("TRN2", target_bir_lowering=False, num_devices=1)
    aps = [nc.dram_tensor(n, v.shape, mybir.dt.from_np(v.dtype), kind="ExternalInput").ap() for n, v in arrays.items()]
    out = nc.dram_tensor("tower_out", (NB, NW, F), F32, kind="ExternalOutput").ap()
    y_stage = [nc.dram_tensor(f"y_stage{i}", (R, 4, H // 2, TG), F16, kind="Internal").ap() for i in range(3)]
    build(nc, *aps, out, y_stage)
    r = run_bass_kernel_spmd(nc, [arrays], core_ids=[0])
    return r.results[0]["tower_out"]
```

```python
from contextlib import ExitStack

import numpy as np
import concourse.bass as bass
from concourse import mybir

ALU = mybir.AluOpType
ACT = mybir.ActivationFunctionType
F32 = mybir.dt.float32
F16 = mybir.dt.float16
I32 = mybir.dt.int32
AX_X = mybir.AxisListType.X

NB, NS = 16, 4000
UP, WIN = 4, 64
HOP = WIN // UP
NW = (UP * (NS - 1) + 1 - WIN) // WIN + 1
P = (NW + 1) // 2
TAP = 2 * HOP + 3
NBIN = WIN // 2 + 1
F, H, E = WIN, 8, 4
R = F // 2
NG = NB // 2
TB = 2 * P
TG = 2 * TB
QSCALE = 64.0
SCORE_SCALE = float(F) ** 0.5 / QSCALE
ALPHA, BETA = 0.12, 0.9
EPS = 1e-5



def columns(sizes):
    at, out = 0, {}
    for name, n in sizes:
        out[name] = (at, at + n)
        at += n
    return out, at


CF, NCF = columns([("ident", 128), ("interp", 128), ("dft", 128), ("fold4", 128), ("minus_low", 1)])
CH, NCH = columns([("ident", 128), ("spread", 4 * 128)])
WA, NWA = columns([("q", H * F), ("k", H * F), ("v", H * F), ("o", H * F)])
WF, NWF = columns([("w1", E * 128 + 128), ("gate", E), ("w2", E * F), ("w2s", 128), ("w3", 3 * F),
                   ("b1", E + 1), ("b2", 3), ("gb", E), ("b3", 2 * F)])
NV = 4 * E + 2


def constants():
    a = -0.75
    cf = np.zeros((128, NCF), np.float32)
    cf[:, slice(*CF["ident"])] = np.eye(128)
    for c in range(2):
        for i in range(HOP):
            for j in range(UP):
                for k in range(4):
                    t = abs(j / UP - (k - 1))
                    w = ((a + 2) * t - (a + 3)) * t * t + 1 if t <= 1 else ((a * t - 5 * a) * t + 8 * a) * t - 4 * a
                    cf[c * HOP + i + k, CF["interp"][0] + c * WIN + UP * i + j] += w
    n = np.arange(WIN)
    for c in range(2):
        at = CF["dft"][0] + c * WIN
        for k in range(NBIN):
            cf[c * WIN + n, at + k] = np.cos(2 * np.pi * n * k / WIN)
        for k in range(1, NBIN - 1):
            cf[c * WIN + n, at + NBIN + k - 1] = np.sin(2 * np.pi * n * k / WIN)
    for r in range(4):
        at = CF["fold4"][0] + r * R
        for k in range(R):
            cf[k, at + k] += 1
            cf[R, at + k] -= 2 if k else 1
            if k:
                cf[F - k, at + k] += 1
    for c in range(2):
        for v in range(2, 4):
            cf[c * NV + v * E:c * NV + v * E + E, CF["minus_low"][0]] = -1
        cf[c * NV + 4 * E + 1, CF["minus_low"][0]] = -1
    ch = np.zeros((128, NCH), np.float16)
    ch[:, slice(*CH["ident"])] = np.eye(128)
    for pair in range(2):
        for c in range(2):
            for v in range(2):
                for e in range(2):
                    at = CH["spread"][0] + (2 * pair + c) * 128 + e * F
                    ch[c * NV + v * E + 2 * pair + e, at:at + F] = 1
    return cf, ch


def build(nc, x, cf_in, ch_in, wa_in, wf_in, out, y_dram):
    with ExitStack() as ctx:
        def sb(name, shape, dt=F32):
            return ctx.enter_context(nc.sbuf_tensor(name, shape, dt))

        def sem(name):
            return ctx.enter_context(nc.semaphore(name))

        cf = sb("cf", [128, NCF])
        ch = sb("ch", [128, NCH], F16)
        wa = sb("wa", [F, NWA])
        wf = sb("wf", [128, NWF])
        area = sb("area", [128, 3 * NB * P + 2 * NB * F])
        tapsT = area[:, 0:NB * P]
        poly = area[:, NB * P:2 * NB * P]
        gauss = area[:, 2 * NB * P:3 * NB * P]
        spec2 = area[0:P, 3 * NB * P:].rearrange("p (t f) -> p t f", f=F)
        H1 = area[:, 0:2 * (E + 1) * TG].rearrange("p (s e n) -> p s e n", s=2, e=E + 1)
        H2 = area[:, 2 * (E + 1) * TG:2 * (E + 4) * TG].rearrange("p (s k n) -> p s k n", s=2, k=3)
        mag = sb("mag", [P, NB * 2, NBIN])
        masked = sb("masked", [P, NB * 2, NBIN])
        dist = sb("dist", [P, NB * 2, NBIN])
        tok = sb("tok", [P, NB * 2, F])
        stat = sb("stat", [P, 3, NB * 2])
        norm = sb("norm", [P, 8, NB * 2])
        xn = sb("xn", [P, NB * 2, R])
        xs = sb("xs", [P, NB * 2, 4 * R], F16)
        half_neg = sb("half_neg", [128, 4])
        wqT = sb("wqT", [F, H, 128])
        wkT = sb("wkT", [F, H, R])
        wvT = sb("wvT", [F, H, R])
        scoreW = sb("scoreW", [128, H, 4, R], F16)
        scoreP = sb("scoreP", [128, H, R], F16)
        outW = sb("outW", [128, 2, F])
        XT = sb("XT", [128, 3, TG], F16)
        YP = sb("YP", [128, 2, 4, TG], F16)
        YS = sb("YS", [128, 3, H, TG], F16)
        xg = sb("xg", [P, 2, 4, R])
        probs = sb("probs", [P, 3, 4, TB])
        ZS = sb("ZS", [128, 2, 2, TG])
        AO = sb("AO", [128, TB])
        h2 = sb("h2", [P, NB * 2, F])
        ln = sb("ln", [P, 4, F])
        lnsq = sb("lnsq", [P, 4, F])
        lnst = sb("lnst", [P, 6, 4])
        x2 = sb("x2", [P, 4, F])
        x2s = sb("x2s", [P, 2, 4, 2 * F], F16)
        X2T = sb("X2T", [128, NG, TG], F16)
        w1h = sb("w1h", [128, E * 128 + 128 + E], F16)
        w1l = sb("w1l", [128, E * 128 + 128 + E], F16)
        b3h = sb("b3h", [2 * NV, 2 * F], F16)
        b3s = sb("b3s", [2 * NV, 2 * F], F16)
        gt = sb("gt", [P, 5, NB, E])
        gs = sb("gs", [P, 8, NB])
        w16 = sb("w16", [P, NB, 2 * NV], F16)
        WT = sb("WT", [2 * NV, NB, P], F16)
        H2r = sb("H2r", [128, 2, 2, TG])
        FO = sb("FO", [128, 2, TB])
        res = sb("res", [P, 2, 2, 2, F])

        ps = ctx.enter_context(nc.psum_tensor("ps", [128, 8, 512], F32))

        def half_bank(n, rows, tiles):
            return ps[0:rows, n, :].bitcast(F16)[:, 0:tiles * 128].rearrange("p (t n) -> p t n", t=tiles)

        ident = cf[:, slice(*CF["ident"])]
        ident16 = ch[:, slice(*CH["ident"])]

        const_in, const16_in, attn_w_in, ffn_w_in = (sem(s) for s in ("const_in", "const16_in", "attn_w_in", "ffn_w_in"))
        taps_in = [sem(f"taps_in{q}") for q in range(4)]
        pad_set, interp_mm, gsq_done, gauss_done, poly_dve = (
            sem(s) for s in ("pad_set", "interp_mm", "gsq_done", "gauss_done", "poly_dve"))
        dft_mm, sq_done, act1, dve1 = (sem(s) for s in ("dft_mm", "sq_done", "act1", "dve1"))
        wfold_mm, wfold_cp, wprod_mm, wprod_cp = (sem(s) for s in ("wfold_mm", "wfold_cp", "wprod_mm", "wprod_cp"))
        xs_done, half_set, square_done = (sem(s) for s in ("xs_done", "half_set", "square_done"))
        xt_mm, xt_cp, y_mm, y_hi, y_lo = (sem(s) for s in ("xt_mm", "xt_cp", "y_mm", "y_hi", "y_lo"))
        y_out = [sem(f"y_out{i}") for i in range(2)]
        y_in = [sem(f"y_in{i}") for i in range(3)]
        xg_cp = sem("xg_cp")
        yd_mm, yd_hi, yd_lo = (sem(s) for s in ("yd_mm", "yd_hi", "yd_lo"))
        s_mm, s_act, z_mm, z_cp = (sem(s) for s in ("s_mm", "s_act", "z_mm", "z_cp"))
        ao_mm, ao_cp, ta_mm, h2_done = (sem(s) for s in ("ao_mm", "ao_cp", "ta_mm", "h2_done"))
        mirrored, packed = sem("mirrored"), sem("packed")
        ln_dve, ln_pool, x2s_done, x2t_mm, x2t_cp = (sem(s) for s in ("ln_dve", "ln_pool", "x2s_done", "x2t_mm", "x2t_cp"))
        w1_split, gate_mm, gate_dve, gate_act, b3_hi = (
            sem(s) for s in ("w1_split", "gate_mm", "gate_dve", "gate_act", "b3_hi"))
        route_done, wt_mm, wt_cp = (sem(s) for s in ("route_done", "wt_mm", "wt_cp"))
        l1_mm, l1_act, l1_dve, l2_mm, l2_act = (sem(s) for s in ("l1_mm", "l1_act", "l1_dve", "l2_mm", "l2_act"))
        wb_mm, mix_done, l3_mm, fo_cp, to_mm, res_done = (
            sem(s) for s in ("wb_mm", "mix_done", "l3_mm", "fo_cp", "to_mm", "res_done"))
        out_done = [sem("out_done0"), sem("out_done1")]

        block = ctx.enter_context(nc.Block())
        unit_of = [(bb, half) for bb in range(2) for half in range(2)]

        @block.sync
        def _(sp):
            for q in range(4):
                cols = slice(4 * q * P, 4 * (q + 1) * P)
                sp.wait_ge(pad_set, q + 1)
                sp.dma_start(tapsT[0:TAP, cols], x[:, cols]).then_inc(taps_in[q], 16)
            sp.dma_start(wf[:], wf_in).then_inc(ffn_w_in, 16)
            for g in range(1, NG):
                for k in range(2):
                    sp.wait_ge(y_lo, 2 * g + k - 1)
                if g >= 4:
                    sp.wait_ge(y_in[g % 3], 32 * ((g - 1) // 3))
                for hh in range(4):
                    sp.dma_start(y_dram[g % 3][:, :, hh, :],
                                 YP[R * hh:R * hh + R, g % 2]).then_inc(y_out[g % 2], 16)
                sp.wait_ge(y_out[g % 2], 64 * ((g + 1) // 2))
                if g >= 3:
                    sp.wait_ge(s_mm, 8 * (g - 2))
                for hl in range(2):
                    stage = y_dram[g % 3]
                    src = bass.AP(stage.tensor, stage.offset + hl * H * TG,
                                  [[0, 2], [2 * H * TG, R], [1, H * TG]])
                    sp.dma_start(YS[64 * hl:64 * hl + 64, g % 3].rearrange("p h n -> p (h n)"), src,
                                 max_dma_last_dim=8192).then_inc(y_in[g % 3], 16)
            for g in range(NG):
                sp.wait_ge(res_done, g + 1)
                for bb in range(2):
                    b = 2 * g + bb
                    sp.dma_start(out[b, 0:NW - 1, :].rearrange("(p c) f -> p c f", c=2),
                                 res[0:P - 1, g % 2, bb]).then_inc(out_done[g % 2], 16)
                sp.dma_start(out[2 * g:2 * g + 2, NW - 1, :].rearrange("(a b) f -> a b f", a=1),
                             res[P - 1:P, g % 2, :, 0, :]).then_inc(out_done[g % 2], 16)
            for k in range(2):
                sp.wait_ge(out_done[k], 48 * (NG // 2))

        @block.tensor
        def _(pe):
            mm = nc.tensor.matmul

            pe.wait_ge(const_in, 16)
            for q in range(4):
                pe.wait_ge(taps_in[q], 16)
                mm(ps[:, 4 + q, 0:4 * P], cf[:, slice(*CF["interp"])], tapsT[:, 4 * q * P:4 * (q + 1) * P],
                   start=True, stop=True).then_inc(interp_mm, 1)
            for q in range(4):
                pe.wait_ge(poly_dve, 2 * q + 2)
                pe.wait_ge(gauss_done, q + 1)
                for i in range(4):
                    b = 4 * q + i
                    for k, part in enumerate((poly, gauss)):
                        t = mm(ps[0:P, q, i * 128:(i + 1) * 128], part[:, b * P:(b + 1) * P],
                               cf[:, slice(*CF["dft"])], start=(k == 0), stop=(k == 1))
                t.then_inc(dft_mm, 1)
            pe.wait_ge(attn_w_in, 16)
            fold4 = cf[0:F, slice(*CF["fold4"])]
            for h in range(H):
                mm(ps[0:F, 4 + h // 4, (h % 4) * 128:(h % 4 + 1) * 128],
                   wa[:, WA["q"][0] + h:WA["q"][1]:H], fold4, start=True, stop=True)
            for h in range(H):
                mm(ps[0:F, 6, h * R:(h + 1) * R], wa[:, WA["k"][0] + h:WA["k"][1]:H], fold4[:, 0:R],
                   start=True, stop=True)
            for h in range(H):
                t = mm(ps[0:F, 7, h * R:(h + 1) * R], wa[:, WA["v"][0] + h:WA["v"][1]:H], fold4[:, 0:R],
                       start=True, stop=True)
            t.then_inc(wfold_mm, 1)
            pe.wait_ge(wfold_cp, 3)
            for h in range(H):
                mm(ps[:, 4 + h // 4, (h % 4) * 128:(h % 4 + 1) * 128].rearrange("p (r f) -> p r f", r=4), wqT[:, h, :],
                   wkT[:, h, :].unsqueeze(1).broadcast_to([F, 4, R]), start=True, stop=True)
            for h in range(H):
                at = R * (h % 4)
                t = mm(ps[at:at + R, 6, (h // 4) * F:(h // 4 + 1) * F], wvT[:, h, :],
                       wa[:, WA["o"][0] + h * F:WA["o"][0] + (h + 1) * F], start=True, stop=True)
            t.then_inc(wprod_mm, 1)

            def x_transpose(g):
                pe.wait_ge(xs_done, 1 if g < 2 else 2)
                if g == 0:
                    pe.wait_ge(const16_in, 16)
                if g >= 1:
                    pe.wait_ge(xt_cp, g)
                if g >= 4:
                    pe.wait_ge(h2_done, g - 3)
                if g >= 5:
                    pe.wait_ge(x2t_cp, g - 4)
                xt = half_bank(7, 128, 4)
                for i in range(4):
                    t = nc.tensor.transpose(xt[:, i, 0:P], xs[:, 4 * g + i, :], ident16[0:P, 0:P])
                t.then_inc(xt_mm, 1)

            def y_project(g, k):
                pe.wait_ge(xt_cp, g + 1)
                if g == 1 and k == 0:
                    pe.wait_ge(packed, 1)
                    pe.wait_ge(yd_lo, H)
                else:
                    pe.wait_ge(y_lo, 2 * g + k - 2)
                mm(ps[:, 6, 0:TG], scoreP[:, 4 * k:4 * k + 4, :].rearrange("p h f -> p (h f)"), XT[:, g % 3, :],
                   start=True, stop=True).then_inc(y_mm, 1)

            def y_direct(h):
                if h == 0:
                    pe.wait_ge(xt_cp, 1)
                    pe.wait_ge(wprod_cp, 4)
                if h >= 2:
                    pe.wait_ge(yd_lo, h - 1)
                mm(ps[:, 5 + h % 2, 0:TG], scoreW[:, h].rearrange("p r f -> p (r f)"), XT[:, 0, :], start=True, stop=True).then_inc(yd_mm, 1)

            def scores(n):
                g, t = divmod(n, 8)
                (bb, half), cj = unit_of[t // 2], t % 2
                if g == 0:
                    pe.wait_ge(yd_lo, 4 * half + 4)
                elif t == 0:
                    pe.wait_ge(y_in[g % 3], 32 * ((g - 1) // 3 + 1))
                if n >= 2:
                    pe.wait_ge(s_act, n - 1)
                for j in range(2):
                    last = mm(ps[0:P, 2 * (n % 2) + j, 0:TG].rearrange("p (h n) -> p h n", h=2),
                              XT[:, g % 3, (2 * bb + cj) * P:(2 * bb + cj + 1) * P],
                              YS[:, g % 3, 4 * half + 2 * j:4 * half + 2 * j + 2, bb * TB:(bb + 1) * TB],
                              start=True, stop=True)
                last.then_inc(s_mm, 1)

            def mix(n):
                g, t = divmod(n, 8)
                u, cj = t // 2, t % 2
                bb, half = unit_of[u]
                keys = P - cj
                pe.wait_ge(s_act, n + 1)
                if t == 0:
                    pe.wait_ge(xg_cp, g + 1)
                if cj == 0 and 4 * g + u >= 2:
                    pe.wait_ge(z_cp, 4 * g + u - 1)
                if n == 2:
                    pe.wait_ge(yd_lo, H)
                for hh in range(4):
                    last = mm(ps[R * hh:R * hh + R, 4 + half, bb * TB:(bb + 1) * TB],
                              xg[0:keys, g % 2, 2 * bb + cj, :], probs[0:keys, n % 3, hh, :],
                              start=(cj == 0), stop=(cj == 1))
                last.then_inc(z_mm, 1)

            def attn_out(g):
                pe.wait_ge(z_cp, 4 * g + 4)
                for c in range(2):
                    for half in range(2):
                        z = ZS[:, g % 2, half, :].rearrange("p (b c n) -> p b c n", b=2, c=2)[:, :, c, :]
                        last = mm(ps[F * c:F * c + F, 7, 0:TB].rearrange("p (b n) -> p b n", b=2),
                                  outW[:, half, :], z, start=(half == 0), stop=(half == 1))
                last.then_inc(ao_mm, 1)

            def attn_out_T(g):
                pe.wait_ge(ao_cp, g + 1)
                for bb in range(2):
                    last = nc.tensor.transpose(ps[0:P, 7, bb * 128:(bb + 1) * 128], AO[:, bb * P:(bb + 1) * P], ident)
                last.then_inc(ta_mm, 1)

            def x2_transpose(g):
                pe.wait_ge(x2s_done, g + 1)
                pe.wait_ge(h2_done, min(g + 2, NG))
                xt = half_bank(7, 128, 4)
                for i in range(4):
                    last = nc.tensor.transpose(xt[:, i, 0:P], x2s[:, g % 2, i, :], ident16[0:P, 0:P])
                last.then_inc(x2t_mm, 1)

            def gates(r):
                bank = 6 + r
                if r == 0:
                    pe.wait_ge(w1_split, 2)
                    pe.wait_ge(y_lo, 2 * NG - 2)
                pe.wait_ge(x2t_cp, 4 * r + 4)
                G0 = E * 128 + 128
                for i in range(NB):
                    row = NB * r + i
                    for k, w in enumerate((w1h, w1l)):
                        last = mm(ps[0:P, bank, i * E:(i + 1) * E], X2T[:, row // 4, (row % 4) * P:(row % 4 + 1) * P],
                                  w[:, G0:G0 + E], start=(k == 0), stop=(k == 1))
                last.then_inc(gate_mm, 1)

            def routing_T(r):
                pe.wait_ge(route_done, r + 1)
                wt = half_bank(6 + r, 2 * NV, 8)
                for b in range(8):
                    last = nc.tensor.transpose(wt[:, b, 0:P], w16[:, 8 * r + b, :], ident16[0:P, 0:P])
                last.then_inc(wt_mm, 1)

            x_transpose(0)
            x_transpose(1)
            for h in range(4):
                y_direct(h)
            for n in range(8 * NG):
                g, t = divmod(n, 8)
                scores(n)
                if n == 0:
                    for h in range(4, H):
                        y_direct(h)
                    for k in range(2):
                        y_project(1, k)
                if t == 0 and g + 2 < NG:
                    x_transpose(g + 2)
                if t == 1 and g + 2 < NG:
                    y_project(g + 2, 0)
                if t == 2 and g >= 1:
                    if g + 2 < NG:
                        pe.wait_ge(xt_cp, g + 3)
                    else:
                        pe.wait_ge(x2t_cp, g - 2)
                    attn_out(g - 1)
                if t == 3 and g + 2 < NG:
                    y_project(g + 2, 1)
                if t == 4 and g >= 1:
                    attn_out_T(g - 1)
                if t == 6 and g >= 2:
                    x2_transpose(g - 2)
                if n == 8 * (NG - 2) + 1:
                    gates(0)
                if n >= 1:
                    mix(n - 1)
            mix(8 * NG - 1)

            def layer1(g, e):
                n = (E + 1) * g + e
                if n >= 3:
                    pg, pu = divmod(n - 3, E + 1)
                    if pu < 3:
                        pe.wait_ge(l1_act, 3 * pg + pu + 1)
                    else:
                        pe.wait_ge(l1_dve, 2 * pg + pu - 2)
                for k, w in enumerate((w1h, w1l)):
                    last = mm(ps[:, n % 3, 0:TG], w[:, e * 128:(e + 1) * 128], X2T[:, g, :],
                              start=(k == 0), stop=(k == 1))
                last.then_inc(l1_mm, 1)

            def layer2(g, k):
                n = 3 * g + k
                if n >= 2:
                    pe.wait_ge(l2_act, n - 1)
                if k < 2:
                    pe.wait_ge(l1_act, 3 * g + (2, 3)[k])
                    if k == 1:
                        pe.wait_ge(l1_dve, 2 * g + 1)
                    for j in range(2):
                        e = 2 * k + j
                        last = mm(ps[F * j:F * j + F, 3 + n % 2, 0:TG],
                                  wf[:, WF["w2"][0] + e * F:WF["w2"][0] + (e + 1) * F], H1[:, g % 2, e, :],
                                  start=True, stop=True)
                else:
                    pe.wait_ge(l1_dve, 2 * g + 2)
                    last = mm(ps[:, 3 + n % 2, 0:TG], wf[:, slice(*WF["w2s"])], H1[:, g % 2, E, :],
                              start=True, stop=True)
                last.then_inc(l2_mm, 1)

            def spread(g, k):
                m = 2 * g + k
                if g % 4 == 0 and k == 0:
                    pe.wait_ge(wt_cp, g // 4 + 1)
                if m >= 1:
                    pe.wait_ge(mix_done, m)
                for c in range(2):
                    at = CH["spread"][0] + (2 * k + c) * 128
                    o = ps[:, 5, 0:TG].rearrange("p (b c n) -> p b c n", b=2, c=2)[:, :, c, :]
                    last = mm(o, ch[0:2 * NV, at:at + 128], WT[:, 2 * g:2 * g + 2, :], start=True, stop=True)
                last.then_inc(wb_mm, 1)

            def layer3(g):
                pe.wait_ge(mix_done, 2 * g + 2)
                pe.wait_ge(l2_act, 3 * g + 3)
                if g >= 1:
                    pe.wait_ge(res_done, g)
                for c in range(2):
                    o = ps[F * c:F * c + F, 6, 0:TB].rearrange("p (b n) -> p b n", b=2)
                    mm(o, b3s[:, c * F:(c + 1) * F], WT[:, 2 * g:2 * g + 2, :], start=True, stop=False)
                for k in range(3):
                    for c in range(2):
                        o = ps[F * c:F * c + F, 6, 0:TB].rearrange("p (b n) -> p b n", b=2)
                        r = H2[:, g % 2, k, :].rearrange("p (b c n) -> p b c n", b=2, c=2)[:, :, c, :]
                        last = mm(o, wf[:, WF["w3"][0] + k * F:WF["w3"][0] + (k + 1) * F], r,
                                  start=False, stop=(k == 2))
                last.then_inc(l3_mm, 1)

            def result_T(g):
                pe.wait_ge(fo_cp, g + 1)
                for bb in range(2):
                    last = nc.tensor.transpose(ps[0:P, 6, bb * 128:(bb + 1) * 128],
                                               FO[:, g % 2, bb * P:(bb + 1) * P], ident)
                last.then_inc(to_mm, 1)

            pe.wait_ge(w1_split, 3)
            pe.wait_ge(s_act, 8 * NG)
            for e in range(3):
                layer1(0, e)
            pe.wait_ge(x2t_cp, NG - 2)
            attn_out(NG - 1)
            for e in range(3, E + 1):
                layer1(0, e)
            routing_T(0)
            for g in range(NG + 2):
                if g < NG:
                    layer2(g, 0)
                    spread(g, 0)
                if g == 0:
                    attn_out_T(NG - 1)
                if g + 1 < NG:
                    layer1(g + 1, 0)
                if g < NG:
                    layer2(g, 1)
                if g + 1 < NG:
                    layer1(g + 1, 1)
                if g < NG:
                    spread(g, 1)
                if g >= 2:
                    result_T(g - 2)
                if g + 1 < NG:
                    layer1(g + 1, 2)
                if g < NG:
                    layer2(g, 2)
                if g == 0:
                    x2_transpose(NG - 2)
                if g == 1:
                    x2_transpose(NG - 1)
                    gates(1)
                if g == 3:
                    routing_T(1)
                if g + 1 < NG:
                    layer1(g + 1, 3)
                if 1 <= g <= NG:
                    layer3(g - 1)
                if g + 1 < NG:
                    layer1(g + 1, 4)

        dve1_at = {}
        gate_at = {}

        class Steps:

            def __init__(self, eng, s):
                self.eng, self.s, self.n = eng, s, 0

            def done(self, ins):
                ins.then_inc(self.s, 1)
                self.n += 1
                return self.n

            def wait(self, n=None):
                self.eng.wait_ge(self.s, self.n if n is None else n)

        @block.vector
        def _(dve):
            v = nc.vector
            for q in range(4):
                v.memset(tapsT[:, 4 * q * P:4 * (q + 1) * P], 0.0).then_inc(pad_set, 1)
            r = 0.5 ** 0.5
            for q in range(4):
                cols = slice(4 * q * P, 4 * (q + 1) * P)
                dve.wait_ge(gsq_done, q + 1)
                v.tensor_scalar(poly[:, cols], ps[:, 4 + q, 0:4 * P], 1.3, r, ALU.add, ALU.mult).then_inc(poly_dve, 1)
                dve.wait_ge(poly_dve, 2 * q + 1)
                v.tensor_tensor(poly[:, cols], poly[:, cols], poly[:, cols], ALU.mult).then_inc(poly_dve, 1)
            st = Steps(dve, dve1)
            halves = (slice(0, NB), slice(NB, 2 * NB))

            def wide(row, rows, n, of=stat):
                return of[:, row, rows].unsqueeze(2).broadcast_to([P, rows.stop - rows.start, n])

            for i, rows in enumerate(halves):
                dve.wait_ge(sq_done, 2 * i + 2)
                dve1_at["power", rows.start] = st.done(
                    v.tensor_tensor(spec2[:, rows, 1:NBIN - 1], spec2[:, rows, 1:NBIN - 1],
                                    spec2[:, rows, NBIN:F], ALU.add))
            for i, rows in enumerate(halves):
                dve.wait_ge(act1, i + 1)
                st.wait(st.done(v.tensor_reduce(stat[:, 2, rows], mag[:, rows, :], AX_X, ALU.max)))
                st.done(v.tensor_scalar(stat[:, 1, rows], stat[:, 2, rows], BETA, None, ALU.mult))
                st.wait(st.done(v.tensor_scalar(stat[:, 0, rows], stat[:, 2, rows], -ALPHA, None, ALU.mult)))
                dve1_at["over", rows.start] = st.done(
                    v.tensor_tensor(masked[:, rows, :], mag[:, rows, :], wide(0, rows, NBIN), ALU.add))
            for i, rows in enumerate(halves):
                dve.wait_ge(act1, i + 3)
                st.wait(st.done(v.tensor_tensor(masked[:, rows, :], masked[:, rows, :], mag[:, rows, :], ALU.mult)))
                dve1_at["dist", rows.start] = st.done(
                    v.tensor_tensor(dist[:, rows, :], masked[:, rows, :], wide(1, rows, NBIN), ALU.subtract))
            for i, rows in enumerate(halves):
                st.done(v.tensor_tensor(masked[:, rows, :], masked[:, rows, :], wide(1, rows, NBIN), ALU.min))

            def soft_minimum(rows):
                n = st.done(v.tensor_tensor(tok[:, rows, 0:NBIN], masked[:, rows, :], dist[:, rows, :], ALU.add))
                st.wait(n)

            def centre(rows):
                st.done(v.tensor_tensor(norm[:, 1, rows], tok[:, rows, 0], tok[:, rows, R], ALU.add))
                st.wait(st.done(v.tensor_reduce(norm[:, 0, rows], tok[:, rows, 0:NBIN], AX_X, ALU.add)))
                st.wait(st.done(v.scalar_tensor_tensor(norm[:, 2, rows], norm[:, 0, rows], 2.0, norm[:, 1, rows],
                                                       ALU.mult, ALU.subtract)))
                dve1_at["centred", rows.start] = st.done(
                    v.scalar_tensor_tensor(mag[:, rows, :], wide(2, rows, NBIN, norm), -1.0 / F,
                                           tok[:, rows, 0:NBIN], ALU.mult, ALU.add))

            def scale(rows):
                st.done(v.tensor_tensor(norm[:, 1, rows], masked[:, rows, 0], masked[:, rows, R], ALU.add))
                st.wait(st.done(v.tensor_reduce(norm[:, 0, rows], masked[:, rows, :], AX_X, ALU.add)))
                st.wait(st.done(v.scalar_tensor_tensor(norm[:, 2, rows], norm[:, 0, rows], 2.0, norm[:, 1, rows],
                                                       ALU.mult, ALU.subtract)))
                st.wait(st.done(v.tensor_scalar(norm[:, 3, rows], norm[:, 2, rows], 1.0 / F, EPS, ALU.mult, ALU.add)))
                st.done(v.tensor_scalar(norm[:, 4, rows], norm[:, 3, rows], -0.5, None, ALU.mult))
                st.wait(st.done(v.tensor_scalar(norm[:, 5, rows].bitcast(I32), norm[:, 3, rows].bitcast(I32),
                                                -0.5, float(0x5F3759DF), ALU.mult, ALU.add)))
                for _ in range(4):
                    st.wait(st.done(v.tensor_tensor(norm[:, 6, rows], norm[:, 5, rows], norm[:, 5, rows], ALU.mult)))
                    st.wait(st.done(v.tensor_tensor(norm[:, 7, rows], norm[:, 6, rows], norm[:, 4, rows], ALU.mult)))
                    st.wait(st.done(v.scalar_tensor_tensor(norm[:, 5, rows], norm[:, 7, rows], 1.5, norm[:, 5, rows],
                                                           ALU.add, ALU.mult)))
                st.wait(st.done(v.tensor_tensor(xn[:, rows, :], mag[:, rows, 0:R], wide(5, rows, R, norm), ALU.mult)))
                for k in (0, 2):
                    n = st.done(v.tensor_copy(xs[:, rows, k * R:(k + 1) * R], xn[:, rows, :]))
                st.wait(n)
                st.done(v.tensor_tensor(xs[:, rows, R:2 * R], xn[:, rows, :], xs[:, rows, 0:R], ALU.subtract))
                v.tensor_tensor(xs[:, rows, 3 * R:4 * R], xn[:, rows, :], xs[:, rows, 0:R],
                                ALU.subtract).then_inc(xs_done, 1)

            first, others = slice(0, 8), slice(8, 2 * NB)
            st.wait()
            dve.wait_ge(act1, 9)
            soft_minimum(first)
            centre(first)
            dve.wait_ge(act1, 10)
            soft_minimum(others)
            dve.wait_ge(square_done, 1)
            scale(first)
            centre(others)
            dve.wait_ge(wprod_cp, 2)
            for k in range(2):
                v.scalar_tensor_tensor(scoreW[F:128, 4 * k:4 * k + 4].rearrange("p h r f -> p (h r f)"),
                                       ps[F:128, 4 + k, :], QSCALE,
                                       scoreW[F:128, 4 * k:4 * k + 4].rearrange("p h r f -> p (h r f)"),
                                       ALU.mult, ALU.subtract).then_inc(wprod_cp, 1)

            def x_take(g):
                dve.wait_ge(xt_mm, g + 1)
                if g >= 3:
                    dve.wait_ge(s_mm, 8 * (g - 2))
                v.tensor_copy(XT[:, g % 3, :].rearrange("p (t n) -> p t n", t=4),
                              half_bank(7, 128, 4)[:, :, 0:P]).then_inc(xt_cp, 1)

            def y_take(g, k):
                m = 2 * g + k - 2
                dve.wait_ge(y_mm, m + 1)
                if g >= 3:
                    dve.wait_ge(y_out[g % 2], 64 * ((g - 1) // 2))
                v.tensor_copy(YP[:, g % 2, k, :], ps[:, 6, 0:TG]).then_inc(y_hi, 1)
                dve.wait_ge(y_hi, m + 1)
                v.tensor_tensor(YP[:, g % 2, 2 + k, :], ps[:, 6, 0:TG], YP[:, g % 2, k, :],
                                ALU.subtract).then_inc(y_lo, 1)

            def z_take(g, u):
                bb, half = unit_of[u]
                dve.wait_ge(z_mm, 8 * g + 2 * u + 2)
                if g >= 2:
                    dve.wait_ge(ao_mm, g - 1)
                v.tensor_copy(ZS[:, g % 2, half, bb * TB:(bb + 1) * TB],
                              ps[:, 4 + half, bb * TB:(bb + 1) * TB]).then_inc(z_cp, 1)

            def ao_take(g):
                dve.wait_ge(ao_mm, g + 1)
                if g >= 1:
                    dve.wait_ge(ta_mm, g)
                v.tensor_copy(AO[:], ps[:, 7, 0:TB]).then_inc(ao_cp, 1)

            def add_attention(g):
                rows = slice(4 * g, 4 * g + 4)
                dve.wait_ge(ta_mm, g + 1)
                dve.wait_ge(mirrored, 2)
                v.scalar_tensor_tensor(h2[:, rows, :], ps[0:P, 7, 0:4 * F].rearrange("p (t f) -> p t f", f=F), 0.0,
                                       tok[:, rows, :], ALU.max, ALU.add).then_inc(h2_done, 1)

            def centre2(g):
                rows = slice(4 * g, 4 * g + 4)
                dve.wait_ge(h2_done, g + 1)
                v.tensor_reduce(lnst[:, 0, :], h2[:, rows, :], AX_X, ALU.add).then_inc(ln_dve, 1)
                dve.wait_ge(ln_dve, 3 * g + 1)
                if g >= 1:
                    dve.wait_ge(x2s_done, g)
                v.scalar_tensor_tensor(ln[:], lnst[:, 0, :].unsqueeze(2).broadcast_to([P, 4, F]), -1.0 / F,
                                       h2[:, rows, :], ALU.mult, ALU.add).then_inc(ln_dve, 1)

            def squares2(g):
                dve.wait_ge(ln_pool, 5 * g + 1)
                v.tensor_reduce(lnst[:, 2, :], lnsq[:], AX_X, ALU.add).then_inc(ln_dve, 1)

            def x2_take(g):
                dve.wait_ge(x2t_mm, g + 1)
                v.tensor_copy(X2T[:, g, :].rearrange("p (t n) -> p t n", t=4),
                              half_bank(7, 128, 4)[:, :, 0:P]).then_inc(x2t_cp, 1)

            def split_weights():
                dve.wait_ge(ffn_w_in, 16)
                v.tensor_copy(w1h[:], wf[:, 0:E * 128 + 128 + E]).then_inc(w1_split, 1)
                dve.wait_ge(w1_split, 1)
                v.tensor_tensor(w1l[:], wf[:, 0:E * 128 + 128 + E], w1h[:], ALU.subtract).then_inc(w1_split, 1)
                b3 = wf[0:2 * NV, slice(*WF["b3"])]
                v.tensor_copy(b3h[:], b3).then_inc(b3_hi, 1)
                dve.wait_ge(b3_hi, 1)
                v.scalar_tensor_tensor(b3s[:], b3h[:], cf[0:2 * NV, slice(*CF["minus_low"])], b3,
                                       ALU.mult, ALU.add).then_inc(w1_split, 1)

            gst = Steps(dve, gate_dve)

            def step(ins):
                gst.wait(gst.done(ins))

            def per_token(row):
                return gs[:, row].unsqueeze(2).broadcast_to([P, NB, E])

            def rank_gates(r):
                if r:
                    dve.wait_ge(wt_mm, r)
                dve.wait_ge(gate_mm, r + 1)
                gb = wf[0:P, slice(*WF["gb"])].unsqueeze(1).broadcast_to([P, NB, E])
                step(v.tensor_tensor(gt[:, 0], ps[0:P, 6 + r, 0:NB * E].rearrange("p (t e) -> p t e", e=E), gb,
                                     ALU.add))
                step(v.tensor_reduce(gs[:, 0], gt[:, 0], AX_X, ALU.max))
                step(v.tensor_tensor(gt[:, 0], gt[:, 0], per_token(0), ALU.subtract))
                gate_at["logits", r] = gst.n
                dve.wait_ge(gate_act, 4 * r + 2)
                step(v.reciprocal(gt[:, 2], gt[:, 2]))
                step(v.tensor_tensor(gt[:, 1], gt[:, 1], gt[:, 2], ALU.mult))
                step(v.tensor_reduce(gs[:, 1], gt[:, 1], AX_X, ALU.add))
                step(v.reciprocal(gs[:, 2], gs[:, 1]))
                step(v.tensor_tensor(gt[:, 1], gt[:, 1], per_token(2), ALU.mult))
                for e in range(E):
                    gst.done(v.memset(gt[:, 0, :, e], float(e)))
                for d in range(1, E):
                    gst.done(v.tensor_tensor(gt[:, 1 + d, :, 0:E - d], gt[:, 1, :, 0:E - d], gt[:, 1, :, d:E], ALU.is_ge))
                gst.wait()
                for d in range(1, E):
                    step(v.tensor_tensor(gt[:, 0, :, 0:E - d], gt[:, 0, :, 0:E - d], gt[:, 1 + d, :, 0:E - d], ALU.add))
                    step(v.tensor_tensor(gt[:, 0, :, d:E], gt[:, 0, :, d:E], gt[:, 1 + d, :, 0:E - d], ALU.subtract))

            def weigh_gates(r):
                gst.done(v.tensor_scalar(gt[:, 2], gt[:, 0], float(E - 1), None, ALU.is_equal))
                step(v.tensor_scalar(gt[:, 3], gt[:, 0], float(E - 2), None, ALU.is_equal))
                gst.done(v.tensor_tensor(gt[:, 4], gt[:, 1], gt[:, 2], ALU.mult))
                step(v.tensor_tensor(gt[:, 0], gt[:, 1], gt[:, 3], ALU.mult))
                step(v.tensor_tensor(gt[:, 4], gt[:, 4], gt[:, 0], ALU.subtract))
                step(v.tensor_reduce(gs[:, 4], gt[:, 4], AX_X, ALU.add))
                gate_at["gap", r] = gst.n
                dve.wait_ge(gate_act, 4 * r + 4)
                gst.done(v.tensor_tensor(gt[:, 2], gt[:, 2], per_token(5), ALU.mult))
                step(v.tensor_tensor(gt[:, 3], gt[:, 3], per_token(6), ALU.mult))
                step(v.tensor_tensor(gt[:, 0], gt[:, 2], gt[:, 3], ALU.add))
                wv = w16[:, 8 * r:8 * r + 8, :].rearrange("p b (c v) -> p (b c) v", c=2)
                for k in (0, 2 * E):
                    gst.done(v.tensor_copy(wv[:, :, k:k + E], gt[:, 0]))
                step(v.memset(wv[:, :, 4 * E:NV], 1.0))
                gst.done(v.tensor_tensor(wv[:, :, E:2 * E], gt[:, 0], wv[:, :, 0:E], ALU.subtract))
                v.tensor_tensor(wv[:, :, 3 * E:4 * E], gt[:, 0], wv[:, :, 0:E], ALU.subtract).then_inc(route_done, 1)

            def routing_take(r):
                dve.wait_ge(wt_mm, r + 1)
                v.tensor_copy(WT[:, 8 * r:8 * r + 8, :], half_bank(6 + r, 2 * NV, 8)[:, :, 0:P]).then_inc(wt_cp, 1)

            x_take(0)
            x_take(1)
            for h in range(H):
                dve.wait_ge(yd_hi, h + 1)
                v.tensor_tensor(YS[F:128, 0, h, :], ps[F:128, 5 + h % 2, 0:TG], YS[F:128, 0, h, :],
                                ALU.subtract).then_inc(yd_lo, 1)
            for k in range(2):
                y_take(1, k)
            dve.wait_ge(square_done, 2)
            scale(others)
            for g in range(NG):
                if g >= 1:
                    z_take(g - 1, 3)
                if g + 2 < NG:
                    x_take(g + 2)
                    y_take(g + 2, 0)
                z_take(g, 0)
                if g >= 1:
                    ao_take(g - 1)
                if g + 2 < NG:
                    y_take(g + 2, 1)
                if g == NG - 2:
                    rank_gates(0)
                z_take(g, 1)
                if g == 0:
                    for rows in (first, others):
                        v.tensor_copy(tok[:, rows, NBIN:F], tok[:, rows, NBIN - 2:0:-1]).then_inc(mirrored, 1)
                if g >= 1:
                    add_attention(g - 1)
                    centre2(g - 1)
                z_take(g, 2)
                if g == 0:
                    split_weights()
                if g >= 1:
                    squares2(g - 1)
                if g >= 2:
                    x2_take(g - 2)
            weigh_gates(0)
            z_take(NG - 1, 3)
            def relu1(g, e):
                n = (E + 1) * g + e
                dve.wait_ge(l1_mm, n + 1)
                if g >= 2:
                    dve.wait_ge(l2_mm, 3 * (g - 1))
                v.tensor_scalar(H1[:, g % 2, e, :], ps[:, n % 3, 0:TG], wf[:, WF["b1"][0] + e:WF["b1"][0] + e + 1],
                                0.0, ALU.add, ALU.max).then_inc(l1_dve, 1)

            def weigh(g, k):
                dve.wait_ge(l2_act, 3 * g + k + 1)
                dve.wait_ge(wb_mm, 2 * g + k + 1)
                if g >= 2:
                    dve.wait_ge(l3_mm, g - 1)
                v.tensor_tensor(H2[:, g % 2, k, :], H2r[:, g % 2, k, :], ps[:, 5, 0:TG], ALU.mult).then_inc(mix_done, 1)

            def fo_take(g):
                dve.wait_ge(l3_mm, g + 1)
                if g >= 2:
                    dve.wait_ge(to_mm, g - 1)
                v.tensor_copy(FO[:, g % 2, :], ps[:, 6, 0:TB]).then_inc(fo_cp, 1)

            def finish(g):
                dve.wait_ge(to_mm, g + 1)
                if g >= 2:
                    dve.wait_ge(out_done[g % 2], 48 * (g // 2))
                v.tensor_tensor(res[:, g % 2].rearrange("p b c f -> p (b c) f"),
                                ps[0:P, 6, 0:4 * F].rearrange("p (t f) -> p t f", f=F),
                                h2[:, 4 * g:4 * g + 4, :], ALU.add).then_inc(res_done, 1)

            ao_take(NG - 1)
            for e in range(3, E + 1):
                relu1(0, e)
            routing_take(0)
            for g in range(NG + 2):
                if g < NG:
                    weigh(g, 0)
                if g == 0:
                    add_attention(NG - 1)
                    centre2(NG - 1)
                if g < NG:
                    weigh(g, 1)
                if g == 0:
                    squares2(NG - 1)
                    x2_take(NG - 2)
                if g >= 2:
                    finish(g - 2)
                if g == 1:
                    x2_take(NG - 1)
                if g == 2:
                    rank_gates(1)
                    weigh_gates(1)
                if g + 1 < NG:
                    relu1(g + 1, 3)
                if 1 <= g <= NG:
                    fo_take(g - 1)
                if g == 3:
                    routing_take(1)
                if g + 1 < NG:
                    relu1(g + 1, 4)

        @block.scalar
        def _(act):
            act.dma_start(cf[:], cf_in).then_inc(const_in, 16)
            act.dma_start(wa[:], wa_in).then_inc(attn_w_in, 16)
            act.dma_start(ch[:], ch_in).then_inc(const16_in, 16)
            fn = nc.scalar.activation
            for q in range(4):
                cols = slice(4 * q * P, 4 * (q + 1) * P)
                act.wait_ge(interp_mm, q + 1)
                fn(gauss[:, cols], ps[:, 4 + q, 0:4 * P], ACT.Square, bias=-0.7).then_inc(gsq_done, 1)
                act.wait_ge(gsq_done, q + 1)
                fn(gauss[:, cols], gauss[:, cols], ACT.Exp, bias=float(np.log(0.5)), scale=-0.5).then_inc(gauss_done, 1)
            for q in range(4):
                act.wait_ge(dft_mm, q + 1)
                fn(spec2[:, 8 * q:8 * q + 8, :], ps[0:P, q, :].rearrange("p (t f) -> p t f", f=F),
                   ACT.Square).then_inc(sq_done, 1)
            halves = (slice(0, NB), slice(NB, 2 * NB))
            for rows in halves:
                act.wait_ge(dve1, dve1_at["power", rows.start])
                fn(mag[:, rows, :], spec2[:, rows, 0:NBIN], ACT.Sqrt).then_inc(act1, 1)
            for rows in halves:
                act.wait_ge(dve1, dve1_at["over", rows.start])
                fn(masked[:, rows, :], masked[:, rows, :], ACT.Sigmoid).then_inc(act1, 1)
            act.wait_ge(wfold_mm, 1)
            fn(wqT[:].rearrange("p (a h) n -> p a (h n)", a=2), ps[0:F, 4:6, :], ACT.Copy).then_inc(wfold_cp, 1)
            for dst, bank in ((wkT, 6), (wvT, 7)):
                fn(dst[:].rearrange("p h n -> p (h n)"), ps[0:F, bank, 0:H * R], ACT.Copy).then_inc(wfold_cp, 1)
            for rows in halves:
                act.wait_ge(dve1, dve1_at["dist", rows.start])
                fn(dist[:, rows, :], dist[:, rows, :], ACT.Abs).then_inc(act1, 1)
            for i, rows in enumerate(halves):
                act.wait_ge(act1, 5 + i)
                fn(dist[:, rows, :], dist[:, rows, :], ACT.Sigmoid).then_inc(act1, 1)
            for i, rows in enumerate(halves):
                act.wait_ge(act1, 7 + i)
                fn(dist[:, rows, :], dist[:, rows, :], ACT.Ln).then_inc(act1, 1)
            act.wait_ge(wprod_mm, 1)
            fn(scoreW[:].rearrange("p (a h) r f -> p a (h r f)", a=2), ps[:, 4:6, :], ACT.Copy,
               scale=QSCALE).then_inc(wprod_cp, 1)
            fn(outW[:].rearrange("p a f -> p (a f)"), ps[:, 6, 0:2 * F], ACT.Copy).then_inc(wprod_cp, 1)
            for rows in (slice(0, 8), slice(8, 2 * NB)):
                act.wait_ge(dve1, dve1_at["centred", rows.start])
                fn(masked[:, rows, :], mag[:, rows, :], ACT.Square).then_inc(square_done, 1)
            for h in range(H):
                act.wait_ge(yd_mm, h + 1)
                fn(YS[:, 0, h, :], ps[:, 5 + h % 2, 0:TG], ACT.Copy).then_inc(yd_hi, 1)
            def gate_sigmoids(r):
                act.wait_ge(gate_dve, gate_at["logits", r])
                fn(gt[:, 1], gt[:, 0], ACT.Sigmoid).then_inc(gate_act, 1)
                fn(gt[:, 2], gt[:, 0], ACT.Sigmoid, scale=-1.0).then_inc(gate_act, 1)

            def gap_sigmoids(r):
                act.wait_ge(gate_dve, gate_at["gap", r])
                fn(gs[:, 5], gs[:, 4], ACT.Sigmoid).then_inc(gate_act, 1)
                fn(gs[:, 6], gs[:, 4], ACT.Sigmoid, scale=-1.0).then_inc(gate_act, 1)

            for n in range(8 * NG):
                act.wait_ge(s_mm, n + 1)
                if n >= 3:
                    act.wait_ge(z_mm, n - 2)
                fn(probs[:, n % 3].rearrange("p (j h) n -> p j (h n)", j=2), ps[0:P, 2 * (n % 2):2 * (n % 2) + 2, 0:TG],
                   ACT.Sigmoid, scale=SCORE_SCALE).then_inc(s_act, 1)
                if n == 8 * (NG - 2) + 3:
                    gate_sigmoids(0)
            gap_sigmoids(0)
            def relu1(g, e):
                n = (E + 1) * g + e
                act.wait_ge(l1_mm, n + 1)
                if g >= 2:
                    act.wait_ge(l2_mm, 3 * (g - 1))
                fn(H1[:, g % 2, e, :], ps[:, n % 3, 0:TG], ACT.Relu,
                   bias=wf[:, WF["b1"][0] + e:WF["b1"][0] + e + 1]).then_inc(l1_act, 1)

            def relu2(g, k):
                n = 3 * g + k
                act.wait_ge(l2_mm, n + 1)
                if g >= 2:
                    act.wait_ge(l3_mm, g - 1)
                dst = H2r[:, g % 2, k, :] if k < 2 else H2[:, g % 2, 2, :]
                fn(dst, ps[:, 3 + n % 2, 0:TG], ACT.Relu,
                   bias=wf[:, WF["b2"][0] + k:WF["b2"][0] + k + 1]).then_inc(l2_act, 1)

            for e in range(3):
                relu1(0, e)
            for g in range(NG):
                for k in range(3):
                    relu2(g, k)
                    if g + 1 < NG:
                        relu1(g + 1, k)
                if g == 2:
                    gate_sigmoids(1)
                    gap_sigmoids(1)

        @block.gpsimd
        def _(pool):
            v = nc.gpsimd
            v.memset(half_neg[:], -0.5).then_inc(half_set, 1)
            pool.wait_ge(half_set, 1)

            def keys(g):
                pool.wait_ge(xs_done, 1 if g < 2 else 2)
                if g >= 2:
                    pool.wait_ge(z_mm, 8 * (g - 1))
                v.tensor_copy(xg[:, g % 2], xn[:, 4 * g:4 * g + 4, :]).then_inc(xg_cp, 1)

            def norm2(g):
                pool.wait_ge(ln_dve, 3 * g + 2)
                v.tensor_tensor(lnsq[:], ln[:], ln[:], ALU.mult).then_inc(ln_pool, 1)
                pool.wait_ge(ln_dve, 3 * g + 3)
                v.tensor_scalar(lnst[:, 3, :], lnst[:, 2, :], 1.0 / F, EPS, ALU.mult, ALU.add).then_inc(ln_pool, 1)
                pool.wait_ge(ln_pool, 5 * g + 2)
                v.tensor_tensor(lnst[:, 4, :], lnst[:, 3, :], half_neg[0:P, 0:4], ALU.pow).then_inc(ln_pool, 1)
                pool.wait_ge(ln_pool, 5 * g + 3)
                v.tensor_tensor(x2[:], ln[:], lnst[:, 4, :].unsqueeze(2).broadcast_to([P, 4, F]),
                                ALU.mult).then_inc(ln_pool, 1)
                pool.wait_ge(ln_pool, 5 * g + 4)
                if g >= 2:
                    pool.wait_ge(x2t_mm, g - 1)
                v.tensor_copy(x2s[:, g % 2, :, 0:F], x2[:]).then_inc(ln_pool, 1)
                pool.wait_ge(ln_pool, 5 * g + 5)
                v.tensor_tensor(x2s[:, g % 2, :, F:2 * F], x2[:], x2s[:, g % 2, :, 0:F],
                                ALU.subtract).then_inc(x2s_done, 1)

            pool.wait_ge(wprod_cp, 4)
            v.tensor_copy(scoreP[:], scoreW[:, :, 0, :]).then_inc(packed, 1)
            keys(0)
            for g in range(NG):
                if g + 1 < NG:
                    keys(g + 1)
                if g >= 1:
                    norm2(g - 1)
            norm2(NG - 1)


def stacked(*blocks):
    return np.concatenate([a for a, n in blocks for _ in range(n)], axis=0)


def kernel(**inputs):
    import concourse.bacc as bacc
    from concourse.bass_utils import run_bass_kernel_spmd

    a = {k: np.asarray(v) for k, v in inputs.items()}
    ffn = {k[len("L0_ffn_"):]: v for k, v in a.items() if k.startswith("L0_ffn_")}
    f32 = np.float32

    wo = a["L0_attn_Wo"].reshape(F, H * F)
    wa = np.concatenate([a["L0_attn_Wq"], a["L0_attn_Wk"], a["L0_attn_Wv"], wo], axis=1)

    wf = np.zeros((128, NWF), f32)

    def put(name, at, rows, block):
        c0 = WF[name][0] + at
        wf[rows:rows + block.shape[0], c0:c0 + block.shape[1]] = block

    for half in range(2):
        for e in range(E):
            put("w1", e * 128, half * F, ffn["eW1"][e])
        put("w1", E * 128, half * F, ffn["sW1"])
        put("gate", 0, half * F, ffn["gW"])
    for e in range(E):
        put("w2", e * F, 0, ffn["eW2"][e])
        put("w3", (e // 2) * F, (e % 2) * F, ffn["eW3"][e])
        put("b1", e, 0, ffn["eb1"][e][:, None])
        put("b2", e // 2, (e % 2) * F, ffn["eb2"][e][:, None])
    put("w2s", 0, 0, ffn["sW2"])
    put("w3", 2 * F, 0, ffn["sW3"])
    put("b1", E, 0, ffn["sb1"][:, None])
    put("b2", 2, 0, ffn["sb2"][:, None])
    put("gb", 0, 0, np.broadcast_to(ffn["gb"][None, :], (128, E)))
    last_bias = stacked((ffn["eb3"], 4), (ffn["sb3"][None, :], 2))
    for c in range(2):
        put("b3", c * F, c * NV, last_bias)

    cf, ch = constants()
    padded = np.pad(a["x"], ((0, 0), (1, 2 * HOP)), mode="edge")
    taps = np.stack([padded[:, s:s + 2 * HOP * P:2 * HOP] for s in range(TAP)])
    arrays = {"x_in": np.ascontiguousarray(taps.reshape(TAP, NB * P)), "cf_in": cf, "ch_in": ch,
              "wa_in": np.ascontiguousarray(wa), "wf_in": wf}
    nc = bacc.Bacc("TRN2", target_bir_lowering=False, num_devices=1)
    aps = [nc.dram_tensor(n, v.shape, mybir.dt.from_np(v.dtype), kind="ExternalInput").ap() for n, v in arrays.items()]
    out = nc.dram_tensor("tower_out", (NB, NW, F), F32, kind="ExternalOutput").ap()
    y_stage = [nc.dram_tensor(f"y_stage{i}", (R, 4, H // 2, TG), F16, kind="Internal").ap() for i in range(3)]
    build(nc, *aps, out, y_stage)
    r = run_bass_kernel_spmd(nc, [arrays], core_ids=[0])
    return r.results[0]["tower_out"]
```

```python
from contextlib import ExitStack

import numpy as np
import concourse.bass as bass
from concourse import mybir

ALU = mybir.AluOpType
ACT = mybir.ActivationFunctionType
F32 = mybir.dt.float32
F16 = mybir.dt.float16
I32 = mybir.dt.int32
AX_X = mybir.AxisListType.X

NB, NS = 16, 4000
UP, WIN = 4, 64
HOP = WIN // UP
NW = (UP * (NS - 1) + 1 - WIN) // WIN + 1
P = (NW + 1) // 2
TAP = 2 * HOP + 3
NBIN = WIN // 2 + 1
F, H, E = WIN, 8, 4
R = F // 2
NG = NB // 2
TB = 2 * P
TG = 2 * TB
QSCALE = 64.0
SCORE_SCALE = float(F) ** 0.5 / QSCALE
ALPHA, BETA = 0.12, 0.9
HEAD_BANK = (2, 3, 5, 6, 4, 7, 5, 4)
EPS = 1e-5
OUT_BANK = (NG - 1) * (6,) + (7,)



def columns(sizes):
    at, out = 0, {}
    for name, n in sizes:
        out[name] = (at, at + n)
        at += n
    return out, at


CF, NCF = columns([("interp", 128), ("ident", 128), ("dft", 128), ("fold4", 128), ("minus_low", 1)])
CH, NCH = columns([("ident", 128), ("spread", 4 * 128)])
WA, NWA = columns([("q", H * F), ("k", H * F), ("v", H * F), ("o", H * F)])
WF, NWF = columns([("w1", E * 128 + 128), ("gate", E), ("w2", E * F), ("w2s", 128), ("w3", 3 * F),
                   ("b1", E + 1), ("b2", 3), ("gb", E), ("b3", 2 * F)])
NV = 4 * E + 2


def constants():
    a = -0.75
    cf = np.zeros((128, NCF), np.float32)
    cf[:, slice(*CF["ident"])] = np.eye(128)
    for c in range(2):
        for i in range(HOP):
            for j in range(UP):
                for k in range(4):
                    t = abs(j / UP - (k - 1))
                    w = ((a + 2) * t - (a + 3)) * t * t + 1 if t <= 1 else ((a * t - 5 * a) * t + 8 * a) * t - 4 * a
                    cf[c * HOP + i + k, CF["interp"][0] + c * WIN + UP * i + j] += w
    n = np.arange(WIN)
    for c in range(2):
        at = CF["dft"][0] + c * WIN
        for k in range(NBIN):
            cf[c * WIN + n, at + k] = np.cos(2 * np.pi * n * k / WIN)
        for k in range(1, NBIN - 1):
            cf[c * WIN + n, at + NBIN + k - 1] = np.sin(2 * np.pi * n * k / WIN)
    for r in range(4):
        at = CF["fold4"][0] + r * R
        for k in range(R):
            cf[k, at + k] += 1
            cf[R, at + k] -= 2 if k else 1
            if k:
                cf[F - k, at + k] += 1
    for c in range(2):
        for v in range(2, 4):
            cf[c * NV + v * E:c * NV + v * E + E, CF["minus_low"][0]] = -1
        cf[c * NV + 4 * E + 1, CF["minus_low"][0]] = -1
    ch = np.zeros((128, NCH), np.float16)
    ch[:, slice(*CH["ident"])] = np.eye(128)
    for pair in range(2):
        for c in range(2):
            for v in range(2):
                for e in range(2):
                    at = CH["spread"][0] + (2 * pair + c) * 128 + e * F
                    ch[c * NV + v * E + 2 * pair + e, at:at + F] = 1
    return cf, ch


def build(nc, x, cf_in, ch_in, wa_in, wf_in, out, y_dram):
    with ExitStack() as ctx:
        def sb(name, shape, dt=F32):
            return ctx.enter_context(nc.sbuf_tensor(name, shape, dt))

        def sem(name):
            return ctx.enter_context(nc.semaphore(name))

        cf = sb("cf", [128, NCF])
        ch = sb("ch", [128, NCH], F16)
        wa = sb("wa", [F, NWA])
        wf = sb("wf", [128, NWF])
        area = sb("area", [128, 3 * NB * P + 2 * NB * F])
        tapsT = area[:, 0:NB * P]
        poly = area[:, NB * P:2 * NB * P]
        gauss = area[:, 2 * NB * P:3 * NB * P]
        spec2 = area[0:P, 3 * NB * P:].rearrange("p (t f) -> p t f", f=F)
        H1 = area[:, 0:2 * (E + 1) * TG].rearrange("p (s e n) -> p s e n", s=2, e=E + 1)
        H2 = area[:, 2 * (E + 1) * TG:2 * (E + 4) * TG].rearrange("p (s k n) -> p s k n", s=2, k=3)
        mag = sb("mag", [P, NB * 2, NBIN])
        masked = sb("masked", [P, NB * 2, NBIN])
        dist = sb("dist", [P, NB * 2, NBIN])
        tok = sb("tok", [P, NB * 2, F])
        stat = sb("stat", [P, 2, NB * 2])
        norm = sb("norm", [P, 8, NB * 2])
        xn = sb("xn", [P, NB * 2, R])
        xs = sb("xs", [P, NB * 2, 4 * R], F16)
        half_neg = sb("half_neg", [128, 2 * NB])
        warm = sb("warm", [128, 128], F16)
        idle = sb("idle", [1, 1])
        wqT = sb("wqT", [F, H, 128])
        wkT = sb("wkT", [F, H, R])
        wvT = sb("wvT", [F, H, R])
        scoreW = sb("scoreW", [128, H, 4, R], F16)
        scoreP = sb("scoreP", [128, H, R], F16)
        outW = sb("outW", [128, 2, F])
        XT = sb("XT", [128, 3, TG], F16)
        YP = sb("YP", [128, 2, 2, 2, TG], F16)
        YS = sb("YS", [128, 3, H, TG], F16)
        probs = sb("probs", [P, 3, 4, TB])
        ZS = sb("ZS", [128, 2, 2, TG])
        AO = sb("AO", [128, TB])
        h2 = sb("h2", [P, NB * 2, F])
        ln = sb("ln", [P, 4, F])
        lnsq = sb("lnsq", [P, 4, F])
        lnst = sb("lnst", [P, 6, 4])
        x2 = sb("x2", [P, 4, F])
        x2s = sb("x2s", [P, 2, 4, 2 * F], F16)
        X2T = sb("X2T", [128, NG, TG], F16)
        w1h = sb("w1h", [128, E * 128 + 128 + E], F16)
        w1l = sb("w1l", [128, E * 128 + 128 + E], F16)
        b3h = sb("b3h", [2 * NV, 2 * F], F16)
        b3s = sb("b3s", [2 * NV, 2 * F], F16)
        gt = sb("gt", [P, 5, NB, E])
        gs = sb("gs", [P, 8, NB])
        w16 = sb("w16", [P, NB, 2 * NV], F16)
        WT = sb("WT", [2 * NV, NB, P], F16)
        H2r = sb("H2r", [128, 2, 2, TG])
        FO = sb("FO", [128, 2, TB])
        res = sb("res", [P, 2, 2, 2, F])

        ps = ctx.enter_context(nc.psum_tensor("ps", [128, 8, 512], F32))

        def half_bank(n, rows, tiles):
            return ps[0:rows, n, :].bitcast(F16)[:, 0:tiles * 128].rearrange("p (t n) -> p t n", t=tiles)

        ident = cf[:, slice(*CF["ident"])]
        ident16 = ch[:, slice(*CH["ident"])]

        interp_in, const_in, const16_in, attn_w_in, ffn_w_in = (
            sem(s) for s in ("interp_in", "const_in", "const16_in", "attn_w_in", "ffn_w_in"))
        taps_in = [sem(f"taps_in{q}") for q in range(4)]
        warm_set, idle_set, pad_set, interp_mm, gsq_done, gauss_done, poly_dve, poly_act, sum_pool, sum_dve = (
            sem(s) for s in ("warm_set", "idle_set", "pad_set", "interp_mm", "gsq_done", "gauss_done", "poly_dve",
                             "poly_act", "sum_pool", "sum_dve"))
        level_pool, over_pool, masked_pool = (sem(s) for s in ("level_pool", "over_pool", "masked_pool"))
        dft_mm, sq_done, act1, dve1 = (sem(s) for s in ("dft_mm", "sq_done", "act1", "dve1"))
        wfold_mm, wfold_cp, wprod_mm, wprod_cp = (sem(s) for s in ("wfold_mm", "wfold_cp", "wprod_mm", "wprod_cp"))
        xn_pool = sem("xn_pool")
        xs0_done, xs_pool, half_set, square_done, rstd_done = (
            sem(s) for s in ("xs0_done", "xs_pool", "half_set", "square_done", "rstd_done"))
        xt_mm, xt_cp, y_mm, y_hi, y_lo = (sem(s) for s in ("xt_mm", "xt_cp", "y_mm", "y_hi", "y_lo"))
        y_out = [sem(f"y_out{i}") for i in range(2)]
        y_in = [sem(f"y_in{i}") for i in range(3)]
        y1_in = [sem(f"y1_in{k}") for k in range(2)]
        yd_mm, yd_hi, yd_lo = (sem(s) for s in ("yd_mm", "yd_hi", "yd_lo"))
        s_mm, s_act, z_mm, z_cp = (sem(s) for s in ("s_mm", "s_act", "z_mm", "z_cp"))
        ao_mm, ao_cp, ta_mm, h2_done = (sem(s) for s in ("ao_mm", "ao_cp", "ta_mm", "h2_done"))
        mirrored, packed = sem("mirrored"), sem("packed")
        ln_dve, ln_pool, x2s_done, x2t_mm, x2t_cp = (sem(s) for s in ("ln_dve", "ln_pool", "x2s_done", "x2t_mm", "x2t_cp"))
        w1_split, gate_mm, gate_dve, gate_act, b3_hi = (
            sem(s) for s in ("w1_split", "gate_mm", "gate_dve", "gate_act", "b3_hi"))
        route_done, wt_mm, wt_cp = (sem(s) for s in ("route_done", "wt_mm", "wt_cp"))
        l1_mm, l1_act, l1_dve, l2_mm, l2_act = (sem(s) for s in ("l1_mm", "l1_act", "l1_dve", "l2_mm", "l2_act"))
        wb_mm, mix_done, l3_mm, fo_cp, to_mm, res_done = (
            sem(s) for s in ("wb_mm", "mix_done", "l3_mm", "fo_cp", "to_mm", "res_done"))
        out_done = [sem("out_done0"), sem("out_done1")]

        block = ctx.enter_context(nc.Block())
        first, others, third, later = slice(0, 8), slice(8, 2 * NB), slice(8, 12), slice(12, 2 * NB)
        middle, last = slice(8, 20), slice(20, 2 * NB)
        unit_of = [(bb, half) for bb in range(2) for half in range(2)]

        def stage_read(eng, g):
            if g == 1:
                for k in range(2):
                    eng.wait_ge(y1_in[k], 32)
            else:
                eng.wait_ge(y_in[g % 3], 32 * ((g - 1) // 3 + (g % 3 != 1)))

        @block.sync
        def _(sp):
            for q in range(4):
                cols = slice(4 * q * P, 4 * (q + 1) * P)
                sp.wait_ge(pad_set, q + 1)
                sp.dma_start(tapsT[0:TAP, cols], x[:, cols]).then_inc(taps_in[q], 16)
            sp.dma_start(wf[:], wf_in).then_inc(ffn_w_in, 16)

            def send(g, k, hl):
                sp.wait_ge((y_hi, y_lo)[hl], 2 * g + k - 1)
                stage = y_dram[g % 3]
                dst = bass.AP(stage.tensor, stage.offset + (hl * H + 4 * k) * TG, [[TG, 4], [2 * H * TG, R], [1, TG]])
                sp.dma_start(dst, YP[:, g % 2, hl, k, :]).then_inc(y_out[g % 2], 16)

            def read_back(g, h0, h1, done):
                stage = y_dram[g % 3]
                for hl in range(2):
                    src = bass.AP(stage.tensor, stage.offset + (hl * H + h0) * TG,
                                  [[0, 2], [2 * H * TG, R], [1, (h1 - h0) * TG]])
                    sp.dma_start(YS[64 * hl:64 * hl + 64, g % 3, h0:h1].rearrange("p h n -> p (h n)"), src,
                                 max_dma_last_dim=8192).then_inc(done, 16)

            for k, hl in ((0, 0), (0, 1), (1, 0)):
                send(1, k, hl)
                if (k, hl) == (1, 0):
                    sp.wait_ge(y_out[1], 48)
                    read_back(1, 0, 4, y1_in[0])
            send(1, 1, 1)
            sp.wait_ge(y_out[1], 64)
            read_back(1, 4, H, y1_in[1])
            for g in range(2, NG):
                for k in range(2):
                    if g >= 4 and k == 0:
                        stage_read(sp, g - 3)
                    for hl in range(2):
                        send(g, k, hl)
                sp.wait_ge(y_out[g % 2], 64 * ((g + 1) // 2))
                if g >= 3:
                    sp.wait_ge(s_mm, 8 * (g - 2))
                read_back(g, 0, H, y_in[g % 3])
            for g in range(NG):
                sp.wait_ge(res_done, g + 1)
                sp.dma_start(out[2 * g:2 * g + 2, 0:NW - 1, :].rearrange("b (p c) f -> p b (c f)", c=2),
                             res[0:P - 1, g % 2].rearrange("p b c f -> p b (c f)")).then_inc(out_done[g % 2], 16)
                sp.dma_start(out[2 * g:2 * g + 2, NW - 1, :].rearrange("(a b) f -> a b f", a=1),
                             res[P - 1:P, g % 2, :, 0, :]).then_inc(out_done[g % 2], 16)
            for k in range(2):
                sp.wait_ge(out_done[k], 32 * (NG // 2))

        @block.tensor
        def _(pe):
            mm = nc.tensor.matmul

            def keep_warm(count):
                for _ in range(count):
                    mm(ps[:, 0, :].rearrange("p (a n) -> p a n", a=4), warm[:],
                       warm[:].unsqueeze(1).broadcast_to([128, 4, 128]), start=True, stop=True)

            pe.wait_ge(warm_set, 1)
            keep_warm(8)
            pe.wait_ge(interp_in, 16)
            for q in range(4):
                pe.wait_ge(taps_in[q], 16)
                mm(ps[:, 4 + q, 0:4 * P], cf[:, slice(*CF["interp"])], tapsT[:, 4 * q * P:4 * (q + 1) * P],
                   start=True, stop=True).then_inc(interp_mm, 1)
            pe.wait_ge(const_in, 16)
            for q in range(4):
                if q < 2:
                    pe.wait_ge(sum_pool, q + 1)
                else:
                    pe.wait_ge(sum_dve, q - 1)
                for i in range(4):
                    b = 4 * q + i
                    t = mm(ps[0:P, q, i * 128:(i + 1) * 128], poly[:, b * P:(b + 1) * P], cf[:, slice(*CF["dft"])],
                           start=True, stop=True)
                t.then_inc(dft_mm, 1)
            pe.wait_ge(attn_w_in, 16)
            fold4 = cf[0:F, slice(*CF["fold4"])]
            for h in range(H):
                mm(ps[0:F, 4 + h // 4, (h % 4) * 128:(h % 4 + 1) * 128],
                   wa[:, WA["q"][0] + h:WA["q"][1]:H], fold4, start=True, stop=True)
            for h in range(H):
                mm(ps[0:F, 6, h * R:(h + 1) * R], wa[:, WA["k"][0] + h:WA["k"][1]:H], fold4[:, 0:R],
                   start=True, stop=True)
            for h in range(H):
                t = mm(ps[0:F, 7, h * R:(h + 1) * R], wa[:, WA["v"][0] + h:WA["v"][1]:H], fold4[:, 0:R],
                       start=True, stop=True)
            t.then_inc(wfold_mm, 1)
            pe.wait_ge(wfold_cp, 3)
            for h in range(H):
                mm(ps[:, 4 + h // 4, (h % 4) * 128:(h % 4 + 1) * 128].rearrange("p (r f) -> p r f", r=4), wqT[:, h, :],
                   wkT[:, h, :].unsqueeze(1).broadcast_to([F, 4, R]), start=True, stop=True)
            for h in range(H):
                at = R * (h % 4)
                t = mm(ps[at:at + R, 6, (h // 4) * F:(h // 4 + 1) * F], wvT[:, h, :],
                       wa[:, WA["o"][0] + h * F:WA["o"][0] + (h + 1) * F], start=True, stop=True)
            t.then_inc(wprod_mm, 1)

            def x_transpose(g):
                if g == 0:
                    pe.wait_ge(xs0_done, 1)
                    pe.wait_ge(const16_in, 16)
                else:
                    pe.wait_ge(xs_pool, g)
                if g >= 1:
                    pe.wait_ge(xt_cp, g)
                if g >= 4:
                    pe.wait_ge(h2_done, g - 3)
                if g >= 5:
                    pe.wait_ge(x2t_cp, g - 4)
                xt = half_bank(7, 128, 4)
                for i in range(4):
                    t = nc.tensor.transpose(xt[:, i, 0:P], xs[:, 4 * g + i, :], ident16[0:P, 0:P])
                t.then_inc(xt_mm, 1)

            def y_project(g, k):
                pe.wait_ge(xt_cp, g + 1)
                if g == 1 and k == 0:
                    pe.wait_ge(packed, 1)
                    pe.wait_ge(yd_lo, 4)
                else:
                    pe.wait_ge(y_lo, 2 * g + k - 2)
                mm(ps[:, 6, 0:TG], scoreP[:, 4 * k:4 * k + 4, :].rearrange("p h f -> p (h f)"), XT[:, g % 3, :],
                   start=True, stop=True).then_inc(y_mm, 1)

            def y_direct(h):
                if h == 0:
                    pe.wait_ge(xt_cp, 1)
                    pe.wait_ge(wprod_cp, 4)
                if h == 5:
                    pe.wait_ge(xt_cp, 2)
                if h >= 6:
                    pe.wait_ge(yd_lo, 3 if h == 6 else 5)
                mm(ps[:, HEAD_BANK[h], 0:TG], scoreW[:, h].rearrange("p r f -> p (r f)"), XT[:, 0, :],
                   start=True, stop=True).then_inc(yd_mm, 1)

            def scores(n):
                g, t = divmod(n, 8)
                (bb, half), cj = unit_of[t // 2], t % 2
                if g == 1 and t in (0, 2):
                    pe.wait_ge(y1_in[t // 2], 32)
                elif g > 1 and t == 0:
                    stage_read(pe, g)
                if n >= 2:
                    pe.wait_ge(s_act, n - 1)
                for j in range(2):
                    if g == 0:
                        pe.wait_ge(yd_lo, 4 * half + 2 * j + 2)
                    last = mm(ps[0:P, 2 * (n % 2) + j, 0:TG].rearrange("p (h n) -> p h n", h=2),
                              XT[:, g % 3, (2 * bb + cj) * P:(2 * bb + cj + 1) * P],
                              YS[:, g % 3, 4 * half + 2 * j:4 * half + 2 * j + 2, bb * TB:(bb + 1) * TB],
                              start=True, stop=True)
                last.then_inc(s_mm, 1)

            def mix(n):
                g, t = divmod(n, 8)
                u, cj = t // 2, t % 2
                bb, half = unit_of[u]
                keys = P - cj
                pe.wait_ge(s_act, n + 1)
                if cj == 0 and 4 * g + u >= 2:
                    pe.wait_ge(z_cp, 4 * g + u - 1)
                if n == 0:
                    pe.wait_ge(yd_lo, H)
                for hh in range(4):
                    last = mm(ps[R * hh:R * hh + R, 4 + half, bb * TB:(bb + 1) * TB],
                              xn[0:keys, 4 * g + 2 * bb + cj, :], probs[0:keys, n % 3, hh, :],
                              start=(cj == 0), stop=(cj == 1))
                last.then_inc(z_mm, 1)

            def attn_out(g):
                pe.wait_ge(z_cp, 4 * g + 4)
                for c in range(2):
                    for half in range(2):
                        z = ZS[:, g % 2, half, :].rearrange("p (b c n) -> p b c n", b=2, c=2)[:, :, c, :]
                        last = mm(ps[F * c:F * c + F, 7, 0:TB].rearrange("p (b n) -> p b n", b=2),
                                  outW[:, half, :], z, start=(half == 0), stop=(half == 1))
                last.then_inc(ao_mm, 1)

            def attn_out_T(g):
                pe.wait_ge(ao_cp, g + 1)
                for bb in range(2):
                    last = nc.tensor.transpose(ps[0:P, 7, bb * 128:(bb + 1) * 128], AO[:, bb * P:(bb + 1) * P], ident)
                last.then_inc(ta_mm, 1)

            def x2_transpose(g):
                pe.wait_ge(x2s_done, g + 1)
                pe.wait_ge(h2_done, min(g + 2, NG))
                if g == NG - 1:
                    pe.wait_ge(x2t_cp, g)
                xt = half_bank(7, 128, 4)
                for i in range(4):
                    last = nc.tensor.transpose(xt[:, i, 0:P], x2s[:, g % 2, i, :], ident16[0:P, 0:P])
                last.then_inc(x2t_mm, 1)

            def gates(r):
                bank = 6 + r
                if r == 0:
                    pe.wait_ge(w1_split, 2)
                    pe.wait_ge(y_lo, 2 * NG - 2)
                pe.wait_ge(x2t_cp, 4 * r + 4)
                G0 = E * 128 + 128
                for i in range(NB):
                    row = NB * r + i
                    for k, w in enumerate((w1h, w1l)):
                        last = mm(ps[0:P, bank, i * E:(i + 1) * E], X2T[:, row // 4, (row % 4) * P:(row % 4 + 1) * P],
                                  w[:, G0:G0 + E], start=(k == 0), stop=(k == 1))
                last.then_inc(gate_mm, 1)

            def routing_T(r):
                pe.wait_ge(route_done, r + 1)
                wt = half_bank(6 + r, 2 * NV, 8)
                for b in range(8):
                    last = nc.tensor.transpose(wt[:, b, 0:P], w16[:, 8 * r + b, :], ident16[0:P, 0:P])
                last.then_inc(wt_mm, 1)

            x_transpose(0)
            for h in range(5):
                y_direct(h)
            x_transpose(1)
            for n in range(8 * NG):
                g, t = divmod(n, 8)
                scores(n)
                if n >= 2:
                    mix(n - 2)
                if n == 0:
                    y_direct(5)
                    y_project(1, 0)
                    y_direct(6)
                    y_direct(7)
                if n == 1:
                    y_project(1, 1)
                if n == 6:
                    x_transpose(2)
                if n in (7, 8):
                    y_project(2, n - 7)
                if t == (3 if g == 1 else 0) and 1 <= g < NG - 2:
                    x_transpose(g + 2)
                if t == (4 if g == 1 else 1) and 1 <= g < NG - 2:
                    y_project(g + 2, 0)
                if t == (5 if g == 1 else 3) and 1 <= g < NG - 2:
                    y_project(g + 2, 1)
                if t == (4 if g == 1 else 2) and g >= 1:
                    if g + 2 < NG:
                        pe.wait_ge(xt_cp, g + 3)
                    else:
                        pe.wait_ge(x2t_cp, g - 2)
                    attn_out(g - 1)
                if t == (7 if g == 1 else 4) and g >= 1:
                    attn_out_T(g - 1)
                if t == 7 and g >= 2:
                    x2_transpose(g - 2)
                if n == 8 * (NG - 2) + 1:
                    gates(0)
            for n in (8 * NG - 2, 8 * NG - 1):
                mix(n)

            def layer1(g, e):
                n = (E + 1) * g + e
                if n >= 3:
                    pg, pu = divmod(n - 3, E + 1)
                    if pu < 3:
                        pe.wait_ge(l1_act, 3 * pg + pu + 1)
                    else:
                        pe.wait_ge(l1_dve, 2 * pg + pu - 2)
                for k, w in enumerate((w1h, w1l)):
                    last = mm(ps[:, n % 3, 0:TG], w[:, e * 128:(e + 1) * 128], X2T[:, g, :],
                              start=(k == 0), stop=(k == 1))
                last.then_inc(l1_mm, 1)

            def layer2(g, k):
                n = 3 * g + k
                if n >= 2:
                    pe.wait_ge(l2_act, n - 1)
                if k < 2:
                    pe.wait_ge(l1_act, 3 * g + (2, 3)[k])
                    if k == 1:
                        pe.wait_ge(l1_dve, 2 * g + 1)
                    for j in range(2):
                        e = 2 * k + j
                        last = mm(ps[F * j:F * j + F, 3 + n % 2, 0:TG],
                                  wf[:, WF["w2"][0] + e * F:WF["w2"][0] + (e + 1) * F], H1[:, g % 2, e, :],
                                  start=True, stop=True)
                else:
                    pe.wait_ge(l1_dve, 2 * g + 2)
                    last = mm(ps[:, 3 + n % 2, 0:TG], wf[:, slice(*WF["w2s"])], H1[:, g % 2, E, :],
                              start=True, stop=True)
                last.then_inc(l2_mm, 1)

            def spread(g, k):
                m = 2 * g + k
                if g % 4 == 0 and k == 0:
                    pe.wait_ge(wt_cp, g // 4 + 1)
                if m >= 1:
                    pe.wait_ge(mix_done, m)
                for c in range(2):
                    at = CH["spread"][0] + (2 * k + c) * 128
                    o = ps[:, 5, 0:TG].rearrange("p (b c n) -> p b c n", b=2, c=2)[:, :, c, :]
                    last = mm(o, ch[0:2 * NV, at:at + 128], WT[:, 2 * g:2 * g + 2, :], start=True, stop=True)
                last.then_inc(wb_mm, 1)

            def layer3(g):
                pe.wait_ge(mix_done, 2 * g + 2)
                pe.wait_ge(l2_act, 3 * g + 3)
                if 1 <= g < NG - 1:
                    pe.wait_ge(res_done, g)
                for c in range(2):
                    o = ps[F * c:F * c + F, OUT_BANK[g], 0:TB].rearrange("p (b n) -> p b n", b=2)
                    mm(o, b3s[:, c * F:(c + 1) * F], WT[:, 2 * g:2 * g + 2, :], start=True, stop=False)
                for k in range(3):
                    for c in range(2):
                        o = ps[F * c:F * c + F, OUT_BANK[g], 0:TB].rearrange("p (b n) -> p b n", b=2)
                        r = H2[:, g % 2, k, :].rearrange("p (b c n) -> p b c n", b=2, c=2)[:, :, c, :]
                        last = mm(o, wf[:, WF["w3"][0] + k * F:WF["w3"][0] + (k + 1) * F], r,
                                  start=False, stop=(k == 2))
                last.then_inc(l3_mm, 1)

            def result_T(g):
                pe.wait_ge(fo_cp, g + 1)
                for bb in range(2):
                    last = nc.tensor.transpose(ps[0:P, OUT_BANK[g], bb * 128:(bb + 1) * 128],
                                               FO[:, g % 2, bb * P:(bb + 1) * P], ident)
                last.then_inc(to_mm, 1)

            pe.wait_ge(w1_split, 3)
            pe.wait_ge(s_act, 8 * NG)
            for e in range(3):
                layer1(0, e)
            pe.wait_ge(x2t_cp, NG - 2)
            attn_out(NG - 1)
            for e in range(3, E + 1):
                layer1(0, e)
            routing_T(0)
            for g in range(NG + 2):
                if g < NG:
                    if g == 4:
                        routing_T(1)
                    layer2(g, 0)
                    if g != 4:
                        spread(g, 0)
                if g == 0:
                    attn_out_T(NG - 1)
                if g + 1 < NG:
                    layer1(g + 1, 0)
                if g == 4:
                    spread(g, 0)
                if g < NG:
                    layer2(g, 1)
                if g + 1 < NG:
                    layer1(g + 1, 1)
                if g == 1:
                    x2_transpose(NG - 1)
                if g < NG:
                    spread(g, 1)
                if g >= 2 and g != NG:
                    result_T(g - 2)
                if g + 1 < NG:
                    layer1(g + 1, 2)
                if g < NG:
                    layer2(g, 2)
                if g == 0:
                    x2_transpose(NG - 2)
                if g == 1:
                    gates(1)
                if g + 1 < NG:
                    layer1(g + 1, 3)
                if 1 <= g <= NG:
                    layer3(g - 1)
                if g == NG:
                    result_T(g - 2)
                if g + 1 < NG:
                    layer1(g + 1, 4)

        def parts(rows):
            n = rows.stop - rows.start
            xr = xs[:, rows, :].rearrange("p t (k a r) -> p t k a r", k=2, a=2)
            return xr[:, :, :, 0, :], xr[:, :, :, 1, :], xn[:, rows, :].unsqueeze(2).broadcast_to([P, n, 2, R])

        dve1_at = {}
        gate_at = {}

        class Steps:

            def __init__(self, eng, s):
                self.eng, self.s, self.n = eng, s, 0

            def done(self, ins):
                ins.then_inc(self.s, 1)
                self.n += 1
                return self.n

            def wait(self, n=None):
                self.eng.wait_ge(self.s, self.n if n is None else n)

        @block.vector
        def _(dve):
            v = nc.vector
            for q in range(4):
                v.memset(tapsT[:, 4 * q * P:4 * (q + 1) * P], 0.0).then_inc(pad_set, 1)
            r = 0.5 ** 0.5
            for q in range(2):
                cols = slice(4 * q * P, 4 * (q + 1) * P)
                dve.wait_ge(gsq_done, q + 1)
                v.tensor_scalar(poly[:, cols], ps[:, 4 + q, 0:4 * P], 1.3, r, ALU.add, ALU.mult).then_inc(poly_dve, 1)
                dve.wait_ge(poly_dve, 2 * q + 1)
                v.tensor_tensor(poly[:, cols], poly[:, cols], poly[:, cols], ALU.mult).then_inc(poly_dve, 1)
            for q in (2, 3):
                cols = slice(4 * q * P, 4 * (q + 1) * P)
                dve.wait_ge(poly_act, q - 1)
                dve.wait_ge(gauss_done, q + 1)
                v.tensor_tensor(poly[:, cols], poly[:, cols], gauss[:, cols], ALU.add).then_inc(sum_dve, 1)
            st = Steps(dve, dve1)

            def wide(row, rows, n, of=stat):
                return of[:, row, rows].unsqueeze(2).broadcast_to([P, rows.stop - rows.start, n])

            for rows in (first, others):
                dve.wait_ge(sq_done, 1 if rows == first else 4)
                dve1_at["power", rows.start] = st.done(
                    v.tensor_tensor(spec2[:, rows, 1:NBIN - 1], spec2[:, rows, 1:NBIN - 1],
                                    spec2[:, rows, NBIN:F], ALU.add))
            for i, rows in enumerate((first, others)):
                dve.wait_ge(act1, i + 1)
                dve1_at["peak", rows.start] = st.done(
                    v.tensor_reduce(stat[:, 0, rows], mag[:, rows, :], AX_X, ALU.max))
                if rows == first:
                    st.wait()
                    dve1_at["over"] = st.done(
                        v.scalar_tensor_tensor(masked[:, rows, :], wide(0, rows, NBIN), -ALPHA, mag[:, rows, :],
                                               ALU.mult, ALU.add))

            def distance(rows):
                dve1_at["dist", rows.start] = st.done(
                    v.scalar_tensor_tensor(dist[:, rows, :], wide(0, rows, NBIN), -BETA, masked[:, rows, :],
                                           ALU.mult, ALU.add))

            def clip(rows):
                st.done(v.scalar_tensor_tensor(masked[:, rows, :], wide(0, rows, NBIN), BETA, masked[:, rows, :],
                                               ALU.mult, ALU.min))

            dve.wait_ge(act1, 3)
            st.wait(st.done(v.tensor_tensor(masked[:, first, :], masked[:, first, :], mag[:, first, :], ALU.mult)))
            distance(first)
            clip(first)
            dve.wait_ge(wfold_mm, 1)
            v.tensor_copy(wqT[:].rearrange("p (a h) n -> p a (h n)", a=2), ps[0:F, 4:6, :]).then_inc(wfold_cp, 1)

            def soft_minimum(rows):
                st.wait()
                dve1_at["token", rows.start] = st.done(
                    v.tensor_tensor(tok[:, rows, 0:NBIN], masked[:, rows, :], dist[:, rows, :], ALU.add))

            def total(rows, of):
                st.wait()
                st.done(v.tensor_tensor(norm[:, 1, rows], of[:, rows, 0], of[:, rows, R], ALU.add))
                st.wait(st.done(v.tensor_reduce(norm[:, 0, rows], of[:, rows, 0:NBIN], AX_X, ALU.add)))
                st.done(v.scalar_tensor_tensor(norm[:, 2, rows], norm[:, 0, rows], 2.0, norm[:, 1, rows],
                                               ALU.mult, ALU.subtract))

            def centre(rows):
                st.wait()
                dve1_at["centred", rows.start] = st.done(
                    v.scalar_tensor_tensor(mag[:, rows, :], wide(2, rows, NBIN, norm), -1.0 / F,
                                           tok[:, rows, 0:NBIN], ALU.mult, ALU.add))

            def square(rows):
                st.wait()
                st.done(v.tensor_tensor(masked[:, rows, :], mag[:, rows, :], mag[:, rows, :], ALU.mult))

            def variance(rows):
                st.wait()
                dve1_at["variance", rows.start] = st.done(
                    v.tensor_scalar(norm[:, 3, rows], norm[:, 2, rows], 1.0 / F, EPS, ALU.mult, ALU.add))

            dve.wait_ge(act1, 6)
            soft_minimum(first)
            total(first, tok)
            centre(first)
            square(first)
            total(first, masked)
            variance(first)
            dve.wait_ge(act1, 7)
            n = st.done(v.tensor_tensor(masked[:, last, :], masked[:, last, :], mag[:, last, :], ALU.mult))
            dve.wait_ge(masked_pool, 1)
            st.wait(n)
            distance(others)
            rows = slice(0, 4)
            dve.wait_ge(rstd_done, 1)
            st.wait(st.done(v.tensor_tensor(xn[:, rows, :], mag[:, rows, 0:R], wide(4, rows, R, norm), ALU.mult)))
            high, low, twice = parts(rows)
            st.wait(st.done(v.tensor_copy(high, twice)))
            v.tensor_tensor(low, twice, high, ALU.subtract).then_inc(xs0_done, 1)
            dve.wait_ge(wprod_cp, 2)
            for k in range(2):
                v.scalar_tensor_tensor(scoreW[F:128, 4 * k:4 * k + 4].rearrange("p h r f -> p (h r f)"),
                                       ps[F:128, 4 + k, :], QSCALE,
                                       scoreW[F:128, 4 * k:4 * k + 4].rearrange("p h r f -> p (h r f)"),
                                       ALU.mult, ALU.subtract).then_inc(wprod_cp, 1)

            def x_take(g):
                dve.wait_ge(xt_mm, g + 1)
                if g >= 3:
                    dve.wait_ge(s_mm, 8 * (g - 2))
                v.tensor_copy(XT[:, g % 3, :].rearrange("p (t n) -> p t n", t=4),
                              half_bank(7, 128, 4)[:, :, 0:P]).then_inc(xt_cp, 1)

            def y_take(g, k):
                m = 2 * g + k - 2
                dve.wait_ge(y_mm, m + 1)
                if g >= 3:
                    dve.wait_ge(y_out[g % 2], 64 * ((g - 1) // 2))
                if g >= 2:
                    v.tensor_copy(YP[:, g % 2, 0, k, :], ps[:, 6, 0:TG]).then_inc(y_hi, 1)
                dve.wait_ge(y_hi, m + 1)
                v.tensor_tensor(YP[:, g % 2, 1, k, :], ps[:, 6, 0:TG], YP[:, g % 2, 0, k, :],
                                ALU.subtract).then_inc(y_lo, 1)

            def z_take(g, u):
                bb, half = unit_of[u]
                dve.wait_ge(z_mm, 8 * g + 2 * u + 2)
                if g >= 2:
                    dve.wait_ge(ao_mm, g - 1)
                v.tensor_copy(ZS[:, g % 2, half, bb * TB:(bb + 1) * TB],
                              ps[:, 4 + half, bb * TB:(bb + 1) * TB]).then_inc(z_cp, 1)

            def ao_take(g):
                dve.wait_ge(ao_mm, g + 1)
                if g >= 1:
                    dve.wait_ge(ta_mm, g)
                v.tensor_copy(AO[:], ps[:, 7, 0:TB]).then_inc(ao_cp, 1)

            def add_attention(g):
                rows = slice(4 * g, 4 * g + 4)
                dve.wait_ge(ta_mm, g + 1)
                dve.wait_ge(mirrored, 2)
                v.scalar_tensor_tensor(h2[:, rows, :], ps[0:P, 7, 0:4 * F].rearrange("p (t f) -> p t f", f=F), 0.0,
                                       tok[:, rows, :], ALU.max, ALU.add).then_inc(h2_done, 1)

            def centre2(g):
                rows = slice(4 * g, 4 * g + 4)
                dve.wait_ge(h2_done, g + 1)
                v.tensor_reduce(lnst[:, 0, :], h2[:, rows, :], AX_X, ALU.add).then_inc(ln_dve, 1)
                dve.wait_ge(ln_dve, 3 * g + 1)
                if g >= 1:
                    dve.wait_ge(x2s_done, g)
                v.scalar_tensor_tensor(ln[:], lnst[:, 0, :].unsqueeze(2).broadcast_to([P, 4, F]), -1.0 / F,
                                       h2[:, rows, :], ALU.mult, ALU.add).then_inc(ln_dve, 1)

            def squares2(g):
                dve.wait_ge(ln_pool, 5 * g + 1)
                v.tensor_reduce(lnst[:, 2, :], lnsq[:], AX_X, ALU.add).then_inc(ln_dve, 1)

            def x2_take(g):
                dve.wait_ge(x2t_mm, g + 1)
                v.tensor_copy(X2T[:, g, :].rearrange("p (t n) -> p t n", t=4),
                              half_bank(7, 128, 4)[:, :, 0:P]).then_inc(x2t_cp, 1)

            gst = Steps(dve, gate_dve)

            def step(ins):
                gst.wait(gst.done(ins))

            def per_token(row):
                return gs[:, row].unsqueeze(2).broadcast_to([P, NB, E])

            def gate_logits(r):
                if r:
                    dve.wait_ge(wt_mm, r)
                dve.wait_ge(gate_mm, r + 1)
                gb = wf[0:P, slice(*WF["gb"])].unsqueeze(1).broadcast_to([P, NB, E])
                step(v.tensor_tensor(gt[:, 0], ps[0:P, 6 + r, 0:NB * E].rearrange("p (t e) -> p t e", e=E), gb,
                                     ALU.add))
                step(v.tensor_reduce(gs[:, 0], gt[:, 0], AX_X, ALU.max))
                gst.done(v.tensor_tensor(gt[:, 0], gt[:, 0], per_token(0), ALU.subtract))
                gate_at["logits", r] = gst.n

            def gate_softmax(r):
                dve.wait_ge(gate_act, 4 * r + 2)
                step(v.reciprocal(gt[:, 2], gt[:, 2]))
                step(v.tensor_tensor(gt[:, 1], gt[:, 1], gt[:, 2], ALU.mult))
                gst.done(v.tensor_reduce(gs[:, 1], gt[:, 1], AX_X, ALU.add))

            def gate_scale(r):
                gst.wait()
                step(v.reciprocal(gs[:, 2], gs[:, 1]))
                gst.done(v.tensor_tensor(gt[:, 1], gt[:, 1], per_token(2), ALU.mult))

            def count_wins(d):
                gst.wait()
                gst.done(v.tensor_tensor(gt[:, 0, :, 0:E - d], gt[:, 0, :, 0:E - d], gt[:, 1 + d, :, 0:E - d], ALU.add))
                gst.wait()
                gst.done(v.tensor_tensor(gt[:, 0, :, d:E], gt[:, 0, :, d:E], gt[:, 1 + d, :, 0:E - d], ALU.subtract))

            def gate_wins_near(r):
                gst.wait()
                for e in range(E):
                    gst.done(v.memset(gt[:, 0, :, e], float(e)))
                for d in range(1, E):
                    gst.done(v.tensor_tensor(gt[:, 1 + d, :, 0:E - d], gt[:, 1, :, 0:E - d], gt[:, 1, :, d:E], ALU.is_ge))
                count_wins(1)

            def gate_wins_far(r):
                for d in range(2, E):
                    count_wins(d)

            def gate_gap(r):
                gst.wait()
                gst.done(v.tensor_scalar(gt[:, 2], gt[:, 0], float(E - 1), None, ALU.is_equal))
                step(v.tensor_scalar(gt[:, 3], gt[:, 0], float(E - 2), None, ALU.is_equal))
                step(v.tensor_tensor(gt[:, 4], gt[:, 2], gt[:, 3], ALU.subtract))
                step(v.tensor_tensor(gt[:, 4], gt[:, 4], gt[:, 1], ALU.mult))
                gst.done(v.tensor_reduce(gs[:, 4], gt[:, 4], AX_X, ALU.add))
                gate_at["gap", r] = gst.n

            def gate_rows(r):
                dve.wait_ge(gate_act, 4 * r + 4)
                gst.done(v.tensor_tensor(gt[:, 2], gt[:, 2], per_token(5), ALU.mult))
                step(v.tensor_tensor(gt[:, 3], gt[:, 3], per_token(6), ALU.mult))
                step(v.tensor_tensor(gt[:, 0], gt[:, 2], gt[:, 3], ALU.add))
                wv = w16[:, 8 * r:8 * r + 8, :].rearrange("p b (c v) -> p (b c) v", c=2)
                for k in (0, 2 * E):
                    gst.done(v.tensor_copy(wv[:, :, k:k + E], gt[:, 0]))
                step(v.memset(wv[:, :, 4 * E:NV], 1.0))
                gst.done(v.tensor_tensor(wv[:, :, E:2 * E], gt[:, 0], wv[:, :, 0:E], ALU.subtract))
                v.tensor_tensor(wv[:, :, 3 * E:4 * E], gt[:, 0], wv[:, :, 0:E], ALU.subtract).then_inc(route_done, 1)

            def routing_take(r):
                dve.wait_ge(wt_mm, r + 1)
                v.tensor_copy(WT[:, 8 * r:8 * r + 8, :], half_bank(6 + r, 2 * NV, 8)[:, :, 0:P]).then_inc(wt_cp, 1)

            def head_low(h):
                dve.wait_ge(yd_hi, h + 1)
                v.tensor_tensor(YS[F:128, 0, h, :], ps[F:128, HEAD_BANK[h], 0:TG], YS[F:128, 0, h, :],
                                ALU.subtract).then_inc(yd_lo, 1)

            x_take(0)
            clip(others)
            for h in range(4):
                head_low(h)
            x_take(1)
            dve.wait_ge(act1, 10)
            soft_minimum(third)
            head_low(4)
            total(third, tok)
            head_low(5)
            centre(third)
            head_low(6)
            y_take(1, 0)
            square(third)
            head_low(7)
            total(third, masked)
            variance(third)
            y_take(1, 1)
            soft_minimum(later)
            z_take(0, 0)
            total(later, tok)
            centre(later)
            z_take(0, 1)
            dve.wait_ge(square_done, 1)
            total(later, masked)
            variance(later)
            z_take(0, 2)
            x_take(2)
            y_take(2, 0)
            y_take(2, 1)
            z_take(0, 3)
            z_take(1, 0)
            x_take(3)
            y_take(3, 0)
            ao_take(0)
            z_take(1, 1)
            y_take(3, 1)
            z_take(1, 2)
            add_attention(0)
            centre2(0)
            for g in range(2, NG):
                if g + 2 < NG:
                    x_take(g + 2)
                z_take(g - 1, 3)
                if g == 2:
                    squares2(0)
                if g + 2 < NG:
                    y_take(g + 2, 0)
                ao_take(g - 1)
                z_take(g, 0)
                if g + 2 < NG:
                    y_take(g + 2, 1)
                if g == NG - 2:
                    gate_logits(0)
                if g == NG - 1:
                    gate_wins_near(0)
                add_attention(g - 1)
                centre2(g - 1)
                if g == NG - 1:
                    gate_wins_far(0)
                z_take(g, 1)
                if g == NG - 1:
                    gate_gap(0)
                squares2(g - 1)
                if g == NG - 2:
                    gate_softmax(0)
                    gate_scale(0)
                z_take(g, 2)
                x2_take(g - 2)
            z_take(NG - 1, 3)
            gate_rows(0)
            def relu1(g, e):
                n = (E + 1) * g + e
                dve.wait_ge(l1_mm, n + 1)
                if g >= 2:
                    dve.wait_ge(l2_mm, 3 * (g - 1))
                v.tensor_scalar(H1[:, g % 2, e, :], ps[:, n % 3, 0:TG], wf[:, WF["b1"][0] + e:WF["b1"][0] + e + 1],
                                0.0, ALU.add, ALU.max).then_inc(l1_dve, 1)

            def weigh(g, k):
                dve.wait_ge(l2_act, 3 * g + k + 1)
                dve.wait_ge(wb_mm, 2 * g + k + 1)
                if g >= 2:
                    dve.wait_ge(l3_mm, g - 1)
                v.tensor_tensor(H2[:, g % 2, k, :], H2r[:, g % 2, k, :], ps[:, 5, 0:TG], ALU.mult).then_inc(mix_done, 1)

            def fo_take(g):
                dve.wait_ge(l3_mm, g + 1)
                if g >= 2:
                    dve.wait_ge(to_mm, g - 1)
                v.tensor_copy(FO[:, g % 2, :], ps[:, OUT_BANK[g], 0:TB]).then_inc(fo_cp, 1)

            def finish(g):
                dve.wait_ge(to_mm, g + 1)
                if g >= 2:
                    dve.wait_ge(out_done[g % 2], 32 * (g // 2))
                v.tensor_tensor(res[:, g % 2].rearrange("p b c f -> p (b c) f"),
                                ps[0:P, OUT_BANK[g], 0:4 * F].rearrange("p (t f) -> p t f", f=F),
                                h2[:, 4 * g:4 * g + 4, :], ALU.add).then_inc(res_done, 1)

            ao_take(NG - 1)
            for e in range(3, E + 1):
                relu1(0, e)
            routing_take(0)
            for g in range(NG + 2):
                if g < NG:
                    weigh(g, 0)
                if g == 0:
                    add_attention(NG - 1)
                    centre2(NG - 1)
                if g == 1:
                    x2_take(NG - 1)
                if g == 2:
                    gate_softmax(1)
                if g == 3:
                    gate_gap(1)
                if g < NG:
                    weigh(g, 1)
                if g == 0:
                    squares2(NG - 1)
                    x2_take(NG - 2)
                if g == 2:
                    gate_scale(1)
                if g >= 2:
                    finish(g - 2)
                if g + 1 < NG:
                    relu1(g + 1, 3)
                if g == 3:
                    gate_rows(1)
                if g == 2:
                    gate_wins_near(1)
                if 1 <= g <= NG:
                    fo_take(g - 1)
                if g == 1:
                    gate_logits(1)
                if g + 1 < NG:
                    relu1(g + 1, 4)
                if g == 2:
                    gate_wins_far(1)
                if g == 3:
                    routing_take(1)

        @block.scalar
        def _(act):
            n_interp = CF["interp"][1]
            act.dma_start(cf[:, 0:n_interp], cf_in[:, 0:n_interp]).then_inc(interp_in, 16)
            act.dma_start(cf[:, n_interp:], cf_in[:, n_interp:]).then_inc(const_in, 16)
            act.dma_start(wa[:], wa_in).then_inc(attn_w_in, 16)
            act.dma_start(ch[:], ch_in).then_inc(const16_in, 16)
            fn = nc.scalar.activation
            r = 0.5 ** 0.5

            def gauss_square(q):
                act.wait_ge(interp_mm, q + 1)
                fn(gauss[:, 4 * q * P:4 * (q + 1) * P], ps[:, 4 + q, 0:4 * P], ACT.Square, bias=-0.7).then_inc(gsq_done, 1)

            def gauss_exp(q):
                cols = slice(4 * q * P, 4 * (q + 1) * P)
                act.wait_ge(gsq_done, q + 1)
                fn(gauss[:, cols], gauss[:, cols], ACT.Exp, bias=float(np.log(0.5)), scale=-0.5).then_inc(gauss_done, 1)

            def poly_square(q):
                fn(poly[:, 4 * q * P:4 * (q + 1) * P], ps[:, 4 + q, 0:4 * P], ACT.Square,
                   bias=1.3 * r, scale=r).then_inc(poly_act, 1)

            gauss_square(0)
            gauss_exp(0)
            gauss_square(1)
            gauss_square(2)
            gauss_exp(1)
            poly_square(2)
            gauss_exp(2)
            gauss_square(3)
            poly_square(3)
            gauss_exp(3)
            act.wait_ge(idle_set, 1)
            fn(idle[:], idle[:], ACT.Sqrt)
            for q in range(4):
                act.wait_ge(dft_mm, q + 1)
                fn(spec2[:, 8 * q:8 * q + 8, :], ps[0:P, q, :].rearrange("p (t f) -> p t f", f=F),
                   ACT.Square).then_inc(sq_done, 1)
            for rows in (first, others):
                act.wait_ge(dve1, dve1_at["power", rows.start])
                fn(mag[:, rows, :], spec2[:, rows, 0:NBIN], ACT.Sqrt).then_inc(act1, 1)

            def distance_terms(rows, n):
                act.wait_ge(dve1, dve1_at["dist", rows.start])
                fn(dist[:, rows, :], dist[:, rows, :], ACT.Abs).then_inc(act1, 1)
                act.wait_ge(act1, n + 1)
                fn(dist[:, rows, :], dist[:, rows, :], ACT.Sigmoid).then_inc(act1, 1)

            def distance_log(rows, n):
                act.wait_ge(act1, n + 2)
                fn(dist[:, rows, :], dist[:, rows, :], ACT.Ln).then_inc(act1, 1)

            act.wait_ge(dve1, dve1_at["over"])
            fn(masked[:, first, :], masked[:, first, :], ACT.Sigmoid).then_inc(act1, 1)
            act.wait_ge(wfold_mm, 1)
            for dst, bank in ((wkT, 6), (wvT, 7)):
                fn(dst[:].rearrange("p h n -> p (h n)"), ps[0:F, bank, 0:H * R], ACT.Copy).then_inc(wfold_cp, 1)
            distance_terms(first, 3)
            distance_log(first, 3)
            act.wait_ge(over_pool, 1)
            fn(masked[:, others, :], masked[:, others, :], ACT.Sigmoid).then_inc(act1, 1)
            act.wait_ge(wprod_mm, 1)
            fn(scoreW[:].rearrange("p (a h) r f -> p a (h r f)", a=2), ps[:, 4:6, :], ACT.Copy,
               scale=QSCALE).then_inc(wprod_cp, 1)
            fn(outW[:].rearrange("p a f -> p (a f)"), ps[:, 6, 0:2 * F], ACT.Copy).then_inc(wprod_cp, 1)
            distance_terms(others, 7)
            distance_log(others, 7)

            def second_high(k):
                act.wait_ge(y_mm, k + 1)
                fn(YP[:, 1, 0, k, :], ps[:, 6, 0:TG], ACT.Copy).then_inc(y_hi, 1)

            def head_high(h):
                act.wait_ge(yd_mm, h + 1)
                fn(YS[:, 0, h, :], ps[:, HEAD_BANK[h], 0:TG], ACT.Copy).then_inc(yd_hi, 1)

            for h in range(5):
                head_high(h)
            fn(idle[:], idle[:], ACT.Sigmoid)

            def gate_sigmoids(r):
                act.wait_ge(gate_dve, gate_at["logits", r])
                fn(gt[:, 1], gt[:, 0], ACT.Sigmoid).then_inc(gate_act, 1)
                fn(gt[:, 2], gt[:, 0], ACT.Sigmoid, scale=-1.0).then_inc(gate_act, 1)

            def gap_sigmoids(r):
                act.wait_ge(gate_dve, gate_at["gap", r])
                fn(gs[:, 5], gs[:, 4], ACT.Sigmoid).then_inc(gate_act, 1)
                fn(gs[:, 6], gs[:, 4], ACT.Sigmoid, scale=-1.0).then_inc(gate_act, 1)

            for n in range(8 * NG):
                act.wait_ge(s_mm, n + 1)
                if n >= 3:
                    act.wait_ge(z_mm, n - 2)
                fn(probs[:, n % 3].rearrange("p (j h) n -> p j (h n)", j=2), ps[0:P, 2 * (n % 2):2 * (n % 2) + 2, 0:TG],
                   ACT.Sigmoid, scale=SCORE_SCALE).then_inc(s_act, 1)
                if n == 0:
                    for h in range(5, H):
                        head_high(h)
                    second_high(0)
                if n == 1:
                    second_high(1)
                if n == 5:
                    act.wait_ge(dve1, dve1_at["centred", later.start])
                    fn(masked[:, later, :], mag[:, later, :], ACT.Square).then_inc(square_done, 1)
                if n == 8 * (NG - 2) + 4:
                    gate_sigmoids(0)
                if n == 8 * (NG - 1) + 7:
                    gap_sigmoids(0)

            def relu1(g, e):
                n = (E + 1) * g + e
                act.wait_ge(l1_mm, n + 1)
                if g >= 2:
                    act.wait_ge(l2_mm, 3 * (g - 1))
                fn(H1[:, g % 2, e, :], ps[:, n % 3, 0:TG], ACT.Relu,
                   bias=wf[:, WF["b1"][0] + e:WF["b1"][0] + e + 1]).then_inc(l1_act, 1)

            def relu2(g, k):
                n = 3 * g + k
                act.wait_ge(l2_mm, n + 1)
                if g >= 2:
                    act.wait_ge(l3_mm, g - 1)
                dst = H2r[:, g % 2, k, :] if k < 2 else H2[:, g % 2, 2, :]
                fn(dst, ps[:, 3 + n % 2, 0:TG], ACT.Relu,
                   bias=wf[:, WF["b2"][0] + k:WF["b2"][0] + k + 1]).then_inc(l2_act, 1)

            for e in range(3):
                relu1(0, e)
            for g in range(NG):
                for k in range(3):
                    relu2(g, k)
                    if g + 1 < NG:
                        relu1(g + 1, k)
                    if g == 1 and k == 2:
                        gate_sigmoids(1)
                    if g == 3 and k == 1:
                        gap_sigmoids(1)

        @block.gpsimd
        def _(pool):
            v = nc.gpsimd
            v.memset(warm[:], 0.0).then_inc(warm_set, 1)
            v.memset(half_neg[:], -0.5).then_inc(half_set, 1)
            v.memset(idle[:], 0.0).then_inc(idle_set, 1)
            for q in range(2):
                cols = slice(4 * q * P, 4 * (q + 1) * P)
                pool.wait_ge(poly_dve, 2 * q + 2)
                pool.wait_ge(gauss_done, q + 1)
                v.tensor_tensor(poly[:, cols], poly[:, cols], gauss[:, cols], ALU.add).then_inc(sum_pool, 1)

            def wide(row, rows, n, of=stat):
                return of[:, row, rows].unsqueeze(2).broadcast_to([P, rows.stop - rows.start, n])

            pool.wait_ge(dve1, dve1_at["peak", others.start])
            v.tensor_scalar(stat[:, 1, others], stat[:, 0, others], -ALPHA, None, ALU.mult).then_inc(level_pool, 1)
            pool.wait_ge(level_pool, 1)
            v.tensor_tensor(masked[:, others, :], wide(1, others, NBIN), mag[:, others, :], ALU.add).then_inc(over_pool, 1)
            pool.wait_ge(half_set, 1)

            def inverse_deviation(rows, of):
                pool.wait_ge(dve1, dve1_at["variance", of.start])
                v.tensor_tensor(norm[:, 4, rows], norm[:, 3, rows], half_neg[0:P, rows],
                                ALU.pow).then_inc(rstd_done, 1)

            def split_rows(g):
                rows = slice(4 * g, 4 * g + 4)
                pool.wait_ge(rstd_done, min(g + 1, 5))
                v.tensor_tensor(xn[:, rows, :], mag[:, rows, 0:R],
                                norm[:, 4, rows].unsqueeze(2).broadcast_to([P, 4, R]), ALU.mult).then_inc(xn_pool, 1)
                high, low, twice = parts(rows)
                pool.wait_ge(xn_pool, 2 * g - 1)
                v.tensor_copy(high, twice).then_inc(xn_pool, 1)
                pool.wait_ge(xn_pool, 2 * g)
                v.tensor_tensor(low, twice, high, ALU.subtract).then_inc(xs_pool, 1)

            def norm2(g):
                pool.wait_ge(ln_dve, 3 * g + 2)
                v.tensor_tensor(lnsq[:], ln[:], ln[:], ALU.mult).then_inc(ln_pool, 1)
                pool.wait_ge(ln_dve, 3 * g + 3)
                v.tensor_scalar(lnst[:, 3, :], lnst[:, 2, :], 1.0 / F, EPS, ALU.mult, ALU.add).then_inc(ln_pool, 1)
                pool.wait_ge(ln_pool, 5 * g + 2)
                v.tensor_tensor(lnst[:, 4, :], lnst[:, 3, :], half_neg[0:P, 0:4], ALU.pow).then_inc(ln_pool, 1)
                pool.wait_ge(ln_pool, 5 * g + 3)
                v.tensor_tensor(x2[:], ln[:], lnst[:, 4, :].unsqueeze(2).broadcast_to([P, 4, F]),
                                ALU.mult).then_inc(ln_pool, 1)
                pool.wait_ge(ln_pool, 5 * g + 4)
                if g >= 2:
                    pool.wait_ge(x2t_mm, g - 1)
                v.tensor_copy(x2s[:, g % 2, :, 0:F], x2[:]).then_inc(ln_pool, 1)
                pool.wait_ge(ln_pool, 5 * g + 5)
                v.tensor_tensor(x2s[:, g % 2, :, F:2 * F], x2[:], x2s[:, g % 2, :, 0:F],
                                ALU.subtract).then_inc(x2s_done, 1)

            pool.wait_ge(act1, 7)
            v.tensor_tensor(masked[:, middle, :], masked[:, middle, :], mag[:, middle, :], ALU.mult).then_inc(masked_pool, 1)
            inverse_deviation(slice(0, 4), first)
            inverse_deviation(slice(4, 8), first)
            split_rows(1)
            pool.wait_ge(wprod_cp, 4)
            v.tensor_copy(scoreP[:], scoreW[:, :, 0, :]).then_inc(packed, 1)
            pool.wait_ge(ffn_w_in, 16)
            v.tensor_copy(w1h[:], wf[:, 0:E * 128 + 128 + E]).then_inc(w1_split, 1)
            pool.wait_ge(w1_split, 1)
            v.tensor_tensor(w1l[:], wf[:, 0:E * 128 + 128 + E], w1h[:], ALU.subtract).then_inc(w1_split, 1)
            b3 = wf[0:2 * NV, slice(*WF["b3"])]
            v.tensor_copy(b3h[:], b3).then_inc(b3_hi, 1)
            pool.wait_ge(b3_hi, 1)
            v.tensor_scalar(b3h[:], b3h[:], cf[0:2 * NV, slice(*CF["minus_low"])], None, ALU.mult).then_inc(b3_hi, 1)
            pool.wait_ge(b3_hi, 2)
            v.tensor_tensor(b3s[:], b3h[:], b3, ALU.add).then_inc(w1_split, 1)
            inverse_deviation(third, third)
            split_rows(2)
            inverse_deviation(slice(12, 16), later)
            split_rows(3)
            inverse_deviation(slice(16, 2 * NB), later)
            for rows in (slice(0, 12), later):
                pool.wait_ge(dve1, dve1_at["token", later.start if rows == later else third.start])
                v.tensor_copy(tok[:, rows, NBIN:F], tok[:, rows, NBIN - 2:0:-1]).then_inc(mirrored, 1)
            for g in range(1, NG):
                if g + 3 < NG:
                    split_rows(g + 3)
                norm2(g - 1)
            norm2(NG - 1)


def stacked(*blocks):
    return np.concatenate([a for a, n in blocks for _ in range(n)], axis=0)


def kernel(**inputs):
    import concourse.bacc as bacc
    from concourse.bass_utils import run_bass_kernel_spmd

    a = {k: np.asarray(v) for k, v in inputs.items()}
    ffn = {k[len("L0_ffn_"):]: v for k, v in a.items() if k.startswith("L0_ffn_")}
    f32 = np.float32

    wo = a["L0_attn_Wo"].reshape(F, H * F)
    wa = np.concatenate([a["L0_attn_Wq"], a["L0_attn_Wk"], a["L0_attn_Wv"], wo], axis=1)

    wf = np.zeros((128, NWF), f32)

    def put(name, at, rows, block):
        c0 = WF[name][0] + at
        wf[rows:rows + block.shape[0], c0:c0 + block.shape[1]] = block

    for half in range(2):
        for e in range(E):
            put("w1", e * 128, half * F, ffn["eW1"][e])
        put("w1", E * 128, half * F, ffn["sW1"])
        put("gate", 0, half * F, ffn["gW"])
    for e in range(E):
        put("w2", e * F, 0, ffn["eW2"][e])
        put("w3", (e // 2) * F, (e % 2) * F, ffn["eW3"][e])
        put("b1", e, 0, ffn["eb1"][e][:, None])
        put("b2", e // 2, (e % 2) * F, ffn["eb2"][e][:, None])
    put("w2s", 0, 0, ffn["sW2"])
    put("w3", 2 * F, 0, ffn["sW3"])
    put("b1", E, 0, ffn["sb1"][:, None])
    put("b2", 2, 0, ffn["sb2"][:, None])
    put("gb", 0, 0, np.broadcast_to(ffn["gb"][None, :], (128, E)))
    last_bias = stacked((ffn["eb3"], 4), (ffn["sb3"][None, :], 2))
    for c in range(2):
        put("b3", c * F, c * NV, last_bias)

    cf, ch = constants()
    padded = np.pad(a["x"], ((0, 0), (1, 2 * HOP)), mode="edge")
    taps = np.stack([padded[:, s:s + 2 * HOP * P:2 * HOP] for s in range(TAP)])
    arrays = {"x_in": np.ascontiguousarray(taps.reshape(TAP, NB * P)), "cf_in": cf, "ch_in": ch,
              "wa_in": np.ascontiguousarray(wa), "wf_in": wf}
    nc = bacc.Bacc("TRN2", target_bir_lowering=False, num_devices=1)
    aps = [nc.dram_tensor(n, v.shape, mybir.dt.from_np(v.dtype), kind="ExternalInput").ap() for n, v in arrays.items()]
    out = nc.dram_tensor("tower_out", (NB, NW, F), F32, kind="ExternalOutput").ap()
    y_stage = [nc.dram_tensor(f"y_stage{i}", (R, 2, H, TG), F16, kind="Internal").ap() for i in range(3)]
    build(nc, *aps, out, y_stage)
    r = run_bass_kernel_spmd(nc, [arrays], core_ids=[0])
    return r.results[0]["tower_out"]
```
